# Optimizing a Trainium2 kernel written in Bass

```python
import numpy as np
import jax
import jax.numpy as jnp

def _softmax(x, axis=-1):
    return jax.nn.softmax(x, axis=axis)

def _gelu(x):
    return jax.nn.gelu(x, approximate=True)

def _silu(x):
    return jax.nn.silu(x)

def _sigmoid(x):
    return jax.nn.sigmoid(x)

def _layernorm(x, axis=-1, eps=1e-05):
    m = jnp.mean(x, axis=axis, keepdims=True)
    v = jnp.var(x, axis=axis, keepdims=True)
    return (x - m) / jnp.sqrt(v + eps)

def _scatter_add(tgt, idx, src, axis=0):
    return tgt.at[idx].add(src)

def _segment_sum(src, seg, n):
    return jax.ops.segment_sum(src, seg, n)
kernel_name = 'mk_macaron_d1_jaxref_r4_e38fba'

def setup_inputs(seed: int=0):
    np.random.seed(seed)
    _w = jnp.asarray

    def _L0_attn_setup():
        import jax, jax.numpy as jnp
        import numpy as np
        EMBED_DIM = 256
        NUM_HEADS = 16
        QKV_DIM = EMBED_DIM // NUM_HEADS
        BATCH = 4
        SEQ_LEN = 512
        key = jax.random.key(seed)
        k_x, k_wqkv, k_wout = jax.random.split(key, 3)
        scale_in = 1.0 / np.sqrt(EMBED_DIM)
        X = jax.random.normal(k_x, (BATCH, SEQ_LEN, EMBED_DIM), dtype=jnp.float32)
        W_qkv = jax.random.normal(k_wqkv, (EMBED_DIM, 3 * EMBED_DIM), dtype=jnp.float32) * scale_in
        b_qkv = jnp.zeros((3 * EMBED_DIM,), dtype=jnp.float32)
        W_out = jax.random.normal(k_wout, (EMBED_DIM, EMBED_DIM), dtype=jnp.float32) * scale_in
        b_out = jnp.zeros((EMBED_DIM,), dtype=jnp.float32)
        return {'X': X, 'W_qkv': W_qkv, 'b_qkv': b_qkv, 'W_out': W_out, 'b_out': b_out}
    _L0_attn_in = _L0_attn_setup()

    def _L0_ffn_setup():
        import jax, jax.numpy as jnp
        import numpy as np
        TOP_K = 2
        key = jax.random.key(seed)
        k1, k2, k3, k4 = jax.random.split(key, 4)
        B, T, D, F, E = (2, 256, 256, 512, 8)
        x = jax.random.normal(k1, (B, T, D), dtype=jnp.float32)
        Wg = jax.random.normal(k2, (D, E), dtype=jnp.float32) * 0.02
        W1 = jax.random.normal(k3, (E, D, F), dtype=jnp.float32) * 0.02
        W2 = jax.random.normal(k4, (E, F, D), dtype=jnp.float32) * 0.02
        return {'x': x, 'Wg': Wg, 'W1': W1, 'W2': W2}
    _L0_ffn_in = _L0_ffn_setup()
    _d = {'L0_attn_X': _L0_attn_in['X'], 'L0_attn_W_qkv': _L0_attn_in['W_qkv'], 'L0_attn_b_qkv': _L0_attn_in['b_qkv'], 'L0_attn_W_out': _L0_attn_in['W_out'], 'L0_attn_b_out': _L0_attn_in['b_out'], 'L0_ffn_Wg': _L0_ffn_in['Wg'], 'L0_ffn_W1': _L0_ffn_in['W1'], 'L0_ffn_W2': _L0_ffn_in['W2']}
    _x0 = _d['L0_attn_X']
    _d['L0_attn_X'] = jax.random.normal(jax.random.fold_in(jax.random.key(seed), 1), (8, 512, 256), dtype=_x0.dtype)
    del _x0
    return _d

def reference(L0_attn_X, L0_attn_W_qkv, L0_attn_b_qkv, L0_attn_W_out, L0_attn_b_out, L0_ffn_Wg, L0_ffn_W1, L0_ffn_W2):

    def _L0_attn_ref(X, W_qkv, b_qkv, W_out, b_out):
        import jax, jax.numpy as jnp
        import numpy as np
        EMBED_DIM = 256
        NUM_HEADS = 16
        QKV_DIM = EMBED_DIM // NUM_HEADS
        BATCH = 4
        SEQ_LEN = 512
        B, S, E = X.shape
        qkv = (jnp.einsum('bse,ef->bsf', X, W_qkv) + b_qkv).reshape(B, S, NUM_HEADS, 3 * QKV_DIM)
        q, k, v = jnp.split(qkv, 3, axis=-1)
        attn = jnp.einsum('bqhd,bkhd->bhqk', q, k) / jnp.sqrt(jnp.float32(QKV_DIM)).astype(X.dtype)
        attn = jax.nn.softmax(attn, axis=-1)
        out = jnp.einsum('bhqk,bkhd->bqhd', attn, v).reshape(B, S, NUM_HEADS * QKV_DIM)
        out = jnp.einsum('bse,ef->bsf', out, W_out) + b_out
        return out

    def _L0_ffn_ref(x, Wg, W1, W2):
        import jax, jax.numpy as jnp
        import numpy as np
        TOP_K = 2
        B, T, D = x.shape
        E = Wg.shape[-1]
        xt = x.reshape(B * T, D)
        logits = xt @ Wg
        probs = jax.nn.softmax(logits, axis=-1)
        topw, topi = jax.lax.top_k(probs, TOP_K)
        topw = topw / jnp.sum(topw, axis=-1, keepdims=True)
        combine = jnp.sum(jax.nn.one_hot(topi, E, dtype=xt.dtype) * topw[..., None], axis=1)
        h = jax.nn.relu(jnp.einsum('nd,edf->enf', xt, W1))
        y = jnp.einsum('enf,efd->end', h, W2)
        out = jnp.einsum('ne,end->nd', combine, y)
        return out.reshape(B, T, D)
    x = L0_attn_X
    x = x + 0.5 * _L0_ffn_ref(_layernorm(x, axis=-1), L0_ffn_Wg, L0_ffn_W1, L0_ffn_W2)
    x = x + _L0_attn_ref(_layernorm(x, axis=-1), L0_attn_W_qkv, L0_attn_b_qkv, L0_attn_W_out, L0_attn_b_out)
    x = x + 0.5 * _L0_ffn_ref(_layernorm(x, axis=-1), L0_ffn_Wg, L0_ffn_W1, L0_ffn_W2)
    return x

_drawn_inputs = setup_inputs


def setup_inputs(seed=0):
    import zlib

    import numpy as np

    out = dict(_drawn_inputs(seed))
    spreads = {'L0_attn_b_qkv': (0.0, 0.1), 'L0_attn_b_out': (0.0, 0.1)}
    factors = {}
    for name, (base, spread) in spreads.items():
        noise = np.random.default_rng([zlib.crc32(name.encode()), seed]).standard_normal(out[name].shape)
        drawn = base * np.exp(spread * noise) if base else spread * noise
        out[name] = jnp.asarray(drawn.astype(out[name].dtype))
    for name, factor in factors.items():
        out[name] = (out[name] * factor).astype(out[name].dtype)
    return out
```

```python
from contextlib import ExitStack

import numpy as np
import concourse.bass as bass
from concourse import mybir

P = 128
F32 = mybir.dt.float32
F32R = mybir.dt.float32r
U32 = mybir.dt.uint32
I32 = mybir.dt.int32
ACT = mybir.ActivationFunctionType
ALU = mybir.AluOpType
AXX = mybir.AxisListType.X
ds = bass.ds


def macaron_kernel(nc, x_in, w_qkv, b_qkv, w_out, b_out, w_gate, w1, w2, out):
    B, S, D = x_in.shape
    E, _, F = w1.shape
    H = 16
    DH = D // H
    TPB = S // P
    T = B * TPB
    DC = D // P
    FC = F // P
    G4 = TPB * E
    REGION = T * P + P
    TILES = -(-(2 * T + E - 1) // 4) * 4
    HU = H // 2
    PAIRS = HU // 2
    VW = DH + 1
    LOGIT_SCALE = 1.0 / float(np.sqrt(DH))
    assert S == 512 and D == 256 and E == 8 and TPB == 4

    x_tok = x_in.rearrange("b (i p) d -> p (b i) d", p=P)
    out_tok = out.rearrange("b (i p) d -> p (b i) d", p=P)

    xs_dram = nc.dram_tensor("xs_lists", [E * REGION, D], F32, kind="Internal").ap()
    y_dram = nc.dram_tensor("y_tiles", [TILES * P, D], F32, kind="Internal").ap()
    qk_dram = nc.dram_tensor("qk_parts", [2, 4, P, S], F32, kind="Internal").ap()

    with ExitStack() as ctx:
        def sb(name, shape, dt=F32):
            return ctx.enter_context(nc.sbuf_tensor(name, shape, dt))

        def sem(name):
            return ctx.enter_context(nc.semaphore(name))

        x = sb("x", [P, T, D])
        w1s = sb("w1s", [P, E, DC, F])
        w2s = sb("w2s", [P, E, FC, D])
        kst = sb("kst", [P, 3, PAIRS, S], F32R)
        qst = sb("qst", [P, 3, PAIRS, S], F32R)
        probs = sb("probs", [P, 8, S])
        vs = sb("vs", [P, 3, TPB, H, VW])
        osb = sb("osb", [P, 2, S])
        attn = sb("attn", [P, 3, TPB, P])
        xT = sb("xT", [P, DC, S])
        wqkv = sb("wqkv", [P, DC, 3, D])
        wout = sb("wout", [P, DC, D])
        wg = sb("wg", [P, DC, E])
        part = sb("part", [P, 4, S], F32R)
        bcol = sb("bcol", [P, 2, 2])
        bv = sb("bv", [P, H, DH])
        bo = sb("bo", [P, D])
        ident = sb("ident", [P, P])
        ones = sb("ones", [P, P])
        upper = sb("upper", [P, P])
        xn_r = sb("xn_r", [P, TPB, D])
        mx = sb("mx", [P, 32])
        mT = sb("mT", [32, P], F32R)
        rs = sb("rs", [P, TPB, 4])
        flat = part[:].bitcast(F32).rearrange("p n s -> p (n s)")
        xn_p = flat[:, 0:TPB * D].rearrange("p (i d) -> p i d", d=D)
        yg = flat[:, TPB * D:2 * TPB * D].rearrange("p (u k d) -> p u k d", u=2, k=2)
        arena = probs[:].rearrange("p a s -> p (a s)")
        xs = arena[:, 0:1024].rearrange("p (r d) -> p r d", r=4)
        xsT = arena[:, 1024:1536].rearrange("p (r d) -> p r d", r=2)
        hid = arena[:, 1536:2560].rearrange("p (r d) -> p r d", r=2)
        hidT = arena[:, 2560:3584].rearrange("p (r d) -> p r d", r=2)
        ysb = attn[:].rearrange("p a q n -> p (a q n)")[:, 0:4 * D].rearrange("p (r d) -> p r d", r=4)
        stats = sb("stats", [P, TPB, 6])
        mv = sb("mv", [P, TPB, 2])
        veps = sb("veps", [P, TPB])
        mhalf = sb("mhalf", [P, TPB])
        rstd = sb("rstd", [P, TPB])
        nmr = sb("nmr", [P, TPB])
        lg = sb("lg", [P, TPB, E])
        m8 = sb("m8", [P, TPB, 8])
        i8 = sb("i8", [P, TPB, 8], U32)
        i8f = sb("i8f", [P, TPB, 2])
        gap = sb("gap", [P, TPB])
        gexp = sb("gexp", [P, TPB])
        gden = sb("gden", [P, TPB])
        grec = sb("grec", [P, TPB])
        wts = sb("wts", [P, T, 2])
        oh = sb("oh", [P, T, 2, E])
        both = sb("both", [P, TPB, E])
        cum = sb("cum", [P, TPB + 1, E])
        rk = sb("rk", [P, T, E])
        rk_base = sb("rk_base", [P, TPB, E])
        pick = sb("pick", [P, TPB, 2, E])
        slot = sb("slot", [P, TPB, 2], U32)
        e_i = sb("e_i", [P, E], I32)
        e_f = sb("e_f", [P, E])
        e_base = sb("e_base", [P, E])
        p_i = sb("p_i", [P, 1], I32)
        p_f = sb("p_f", [P, 1])
        j_f = sb("j_f", [P, TILES])
        cnt = sb("cnt", [P, E])
        cnt_i = sb("cnt_i", [P, E], I32)
        nt = sb("nt", [P, E])
        zero8 = sb("zero8", [P, E])
        ends = sb("ends", [P, E])
        start128 = sb("start128", [P, E])
        abase = sb("abase", [P, E])
        dbase = sb("dbase", [P, E])
        padf = sb("padf", [P, E])
        pad = sb("pad", [P, E], U32)
        exp_tab = sb("exp_tab", [P, TILES], I32)
        row_tab = sb("row_tab", [P, TILES], I32)
        yslot = sb("yslot", [P, T, 2], U32)
        yidx = sb("yidx", [P, 2, 2], U32)

        ps = ctx.enter_context(nc.psum_tensor("ps", [P, 8, 512], F32))
        O_BANK, T_BANK = 6, 7

        zrows = probs[:, 0, 0:D]
        rk_y = probs[:, 1, 0:T * E].rearrange("p (t e) -> p t e", e=E)
        pick_y = probs[:, 2, 0:T * 2 * E].rearrange("p (t k e) -> p t k e", k=2, e=E)
        lep = probs[:, 3:5, :].rearrange("p a s -> p (a s)")[:, 0:TILES * E].rearrange("p (j e) -> p j e", e=E)

        le = probs[:, 5:7, :].rearrange("p a s -> p (a s)")[:, 0:TILES * E].rearrange("p (j e) -> p j e", e=E)
        ef, rowf, tmpj = (probs[:, 7, n * TILES:(n + 1) * TILES] for n in range(3))
        wraw = arena[:, 0:DC * 3 * D].rearrange("p (c n) -> p c n", c=DC)
        j_i = probs[:, 7, 3 * TILES:4 * TILES].bitcast(I32)

        s_x = sem("x_loaded")
        s_w = sem("ffn_weights_loaded")
        s_small = sem("small_weights_loaded")
        s_sorted = sem("qkv_columns_sorted")
        s_iota = sem("iotas_made")
        s_const = sem("constants_made")
        s_dve0 = sem("dve_constants_made")

        class Norm:

            def __init__(self, n):
                self.stats = sem(n + "_stats")
                self.mv = sem(n + "_mean_var")
                self.veps = sem(n + "_var_eps")
                self.rstd = sem(n + "_rstd")
                self.nmr = sem(n + "_neg_mean_rstd")
                self.xn = sem(n + "_rows")
                self.tp = sem(n + "_transposed")
                self.ev0 = sem(n + "_chunk0_copied")
                self.ev1 = sem(n + "_chunk1_copied")

        class Route:

            def __init__(self, n):
                self.norm = Norm(n)
                self.lg = sem(n + "_logits")
                self.d = sem(n + "_dve_step")
                self.gap = sem(n + "_gap_ready")
                self.exp = sem(n + "_gap_exp")
                self.cum = sem(n + "_counts_ready")
                self.rank = sem(n + "_ranks")
                self.slot = sem(n + "_slots")
                self.sent = sem(n + "_rows_sent")
                self.free = sem(n + "_rows_free")
                self.total = sem(n + "_totals")
                self.t = sem(n + "_table_step")
                self.tabs = sem(n + "_tables_ready")
                self.zero = sem(n + "_zero_rows")
                self.pad = sem(n + "_pads_sent")
                self.pad_ready = sem(n + "_pad_rows_ready")

        class Expert:

            def __init__(self, n):
                self.ld = [sem(f"{n}_rows_loaded{r}") for r in range(4)]
                self.tp = sem(n + "_rows_transposed")
                self.xT = sem(n + "_rowsT_copied")
                self.h = sem(n + "_hidden_made")
                self.relu = sem(n + "_hidden_relu")
                self.hTp = sem(n + "_hidden_transposed")
                self.hT = sem(n + "_hiddenT_copied")
                self.y = sem(n + "_y_made")
                self.ysb = sem(n + "_y_copied")
                self.st = [sem(f"{n}_y_stored{r}") for r in range(4)]

        r0, r1 = Route("r0"), Route("r1")
        npr = Norm("pr")
        x0, x1 = Expert("x0"), Expert("x1")
        s_gath = [[sem(f"gathered{l}_{r}") for r in range(2)] for l in range(2)]
        s_idx = [sem(f"gather_rows{l}") for l in range(2)]
        s_comb = [sem(f"combined{l}") for l in range(2)]
        s_comb_half = [sem(f"combined_half{l}") for l in range(2)]
        s_qk = sem("qk_products")
        s_hi = sem("qk_hi")
        s_lo = sem("qk_lo")
        s_v = sem("v_products")
        s_vs = sem("v_copied")
        s_part = sem("parts_stored")
        s_ld = [sem(f"stack_loaded{c}") for c in range(2)]
        s_bias = sem("out_bias_added")
        s_mm = sem("max_scores")
        s_red = sem("max_reduced")
        s_mtr = sem("max_transposed")
        s_mev = sem("max_negated")
        s_mrow = [sem(f"max_row_placed{c}") for c in range(2)]
        s_sc = sem("scores")
        s_exp = sem("exps")
        s_pv = sem("pv")
        s_oev = sem("heads_copied")
        s_otr = sem("heads_transposed")
        s_rec = sem("sums_inverted")
        s_at = sem("heads_normalised")
        s_ptr = sem("attn_transposed")
        s_pev0 = sem("attnT0_copied")
        s_pev1 = sem("attnT1_copied")
        s_prj = sem("projected")
        s_x2 = sem("attention_added")
        s_out = sem("out_stored")

        NCONST = 8

        block = ctx.enter_context(nc.Block())

        def apart(eng):
            eng.nop(nofuse=True)

        def batch_rows(b, i=0, n=1):
            return x[:, ds(b * TPB + i, n), :]

        def dve_norm(eng, n, b, xn, xn_free=None):
            apart(eng)
            for i in range(TPB):
                nc.vector.bn_stats(stats[:, i, :], x[:, ds(b * TPB + i, 1), :].rearrange("p o d -> p (o d)")
                                   ).then_inc(n.stats, 1)
            eng.wait_ge(n.stats, TPB * b + TPB)
            apart(eng)
            for i in range(TPB):
                nc.vector.bn_aggr(mv[:, i, :], stats[:, i, :]).then_inc(n.mv, 1)
            eng.wait_ge(n.mv, TPB * b + TPB)
            nc.vector.tensor_scalar(veps[:], mv[:, :, 1], 1e-5, None, ALU.add).then_inc(n.veps, 1)
            eng.wait_ge(n.rstd, b + 1)
            nc.vector.scalar_tensor_tensor(nmr[:], mv[:, :, 0], -1.0, rstd[:], ALU.mult, ALU.mult
                                           ).then_inc(n.nmr, 1)
            if xn_free is not None:
                xn_free()
            eng.wait_ge(n.nmr, b + 1)
            for i in range(TPB):
                nc.vector.tensor_scalar(xn[:, i, :], x[:, ds(b * TPB + i, 1), :].rearrange("p o d -> p (o d)"),
                                        rstd[:, i:i + 1], nmr[:, i:i + 1], ALU.mult, ALU.add
                                        ).then_inc(n.xn, 1)

        def pool_norm(eng, n, b):
            eng.wait_ge(n.veps, b + 1)
            nc.gpsimd.tensor_tensor(rstd[:], veps[:], mhalf[:], ALU.pow).then_inc(n.rstd, 1)

        def pe_norm(eng, n, b, xn):
            eng.wait_ge(n.xn, TPB * b + TPB)
            for c in range(DC):
                for i in range(TPB):
                    mm = nc.tensor.transpose(ps[:, c, i * P:(i + 1) * P], xn[:, i, c * P:(c + 1) * P], ident[:])
                mm.then_inc(n.tp, 1)

        def act_norm(eng, n, b):
            eng.wait_ge(n.tp, 2 * b + 1)
            nc.scalar.copy(xT[:, 0, :], ps[:, 0, :]).then_inc(n.ev0, 1)

        def dve_norm_copy(eng, n, b):
            eng.wait_ge(n.tp, 2 * b + 2)
            nc.vector.tensor_copy(xT[:, 1, :], ps[:, 1, :]).then_inc(n.ev1, 1)

        def pe_route(eng, r, b, xn):
            eng.wait_ge(r.norm.ev0, b + 1)
            eng.wait_ge(r.norm.ev1, b + 1)
            for i in range(TPB):
                for c in range(DC):
                    mm = nc.tensor.matmul(ps[:, 2, i * E:(i + 1) * E], xT[:, c, i * P:(i + 1) * P], wg[:, c, :],
                                          start=(c == 0), stop=(c == DC - 1))
            mm.then_inc(r.lg, 1)
            eng.wait_ge(r.cum, TPB * b + TPB)
            for i in range(TPB):
                nc.tensor.matmul(ps[:, 3, i * E:(i + 1) * E], upper[:], both[:, i, :], start=True, stop=False)
                mm = nc.tensor.matmul(ps[:, 3, i * E:(i + 1) * E], ones[:], cum[:, i, :], start=False, stop=True)
            mm.then_inc(r.rank, 1)

        def act_route(eng, r, b):
            eng.wait_ge(r.gap, b + 1)
            nc.scalar.activation(gexp[:], gap[:], ACT.Exp).then_inc(r.exp, 1)

        NSTEP = 2 * TPB + 6

        def dve_route(eng, r, b, first=False):
            eng.wait_ge(r.lg, b + 1)
            base = NSTEP * b
            nc.vector.tensor_copy(lg[:], ps[:, 2, 0:G4].rearrange("p (i e) -> p i e", e=E)).then_inc(r.d, 1)
            eng.wait_ge(r.d, base + 1)
            apart(eng)
            for i in range(TPB):
                nc.vector.max(m8[:, i, :], lg[:, i, :]).then_inc(r.d, 1)
            eng.wait_ge(r.d, base + 1 + TPB)
            apart(eng)
            for i in range(TPB):
                nc.vector.max_index(i8[:, i, :], m8[:, i, :], lg[:, i, :]).then_inc(r.d, 1)
            nc.vector.tensor_tensor(gap[:], m8[:, :, 1], m8[:, :, 0], ALU.subtract).then_inc(r.gap, 1)
            eng.wait_ge(r.d, base + 1 + 2 * TPB)
            nc.vector.tensor_copy(i8f[:], i8[:, :, 0:2]).then_inc(r.d, 1)
            eng.wait_ge(r.d, base + 2 + 2 * TPB)
            ohb = oh[:, ds(b * TPB, TPB), :, :]
            nc.vector.tensor_tensor(
                ohb, i8f[:].unsqueeze(3).broadcast_to([P, TPB, 2, E]),
                e_f[:].unsqueeze(1).unsqueeze(1).broadcast_to([P, TPB, 2, E]), ALU.is_equal).then_inc(r.d, 1)
            eng.wait_ge(r.d, base + 3 + 2 * TPB)
            ohb0 = oh[:, ds(b * TPB, TPB), 0:1, :].rearrange("p i o e -> p i (o e)")
            ohb1 = oh[:, ds(b * TPB, TPB), 1:2, :].rearrange("p i o e -> p i (o e)")
            nc.vector.tensor_tensor(both[:], ohb0, ohb1, ALU.add).then_inc(r.d, 1)
            eng.wait_ge(r.d, base + 4 + 2 * TPB)
            for i in range(TPB):
                nc.vector.tensor_tensor(cum[:, i + 1, :], cum[:, i, :], both[:, i, :], ALU.add).then_inc(r.cum, 1)
                eng.wait_ge(r.cum, TPB * b + i + 1)
            eng.wait_ge(r.exp, b + 1)
            nc.vector.tensor_scalar(gden[:], gexp[:], 2.0, 2.0, ALU.mult, ALU.add).then_inc(r.d, 1)
            eng.wait_ge(r.d, base + 5 + 2 * TPB)
            nc.vector.reciprocal(grec[:], gden[:]).then_inc(r.d, 1)
            eng.wait_ge(r.d, base + 6 + 2 * TPB)
            apart(eng)
            nc.vector.tensor_copy(wts[:, ds(b * TPB, TPB), 0:1], grec[:].unsqueeze(2))
            nc.vector.tensor_tensor(wts[:, ds(b * TPB, TPB), 1:2], grec[:].unsqueeze(2), gexp[:].unsqueeze(2),
                                    ALU.mult).then_inc(r.slot, 1)
            eng.wait_ge(r.rank, b + 1)
            apart(eng)
            rkv = ps[:, 3, 0:G4].rearrange("p (i e) -> p i e", e=E)
            nc.vector.tensor_copy(rk[:, ds(b * TPB, TPB), :], rkv).then_inc(r.slot, 1)
            nc.vector.tensor_tensor(rk_base[:], rkv, e_base[:].unsqueeze(1).broadcast_to([P, TPB, E]), ALU.add
                                    ).then_inc(r.slot, 1)
            nc.vector.tensor_copy(cum[:, 0, :], cum[:, TPB, :]).then_inc(r.slot, 1)
            eng.wait_ge(r.slot, 6 * b + 4)
            nc.vector.tensor_tensor(pick[:], ohb, rk_base[:].unsqueeze(2).broadcast_to([P, TPB, 2, E]), ALU.mult
                                    ).then_inc(r.slot, 1)
            eng.wait_ge(r.slot, 6 * b + 5)
            if live_b(b, 1):
                if r is r0:
                    eng.wait_ge(r.sent, SENT * b)
                else:
                    eng.wait_ge(r.free, b + 1)
            with nc.allow_low_precision(reason="row numbers below 2**24, exact in float32"):
                nc.vector.tensor_reduce(slot[:], pick[:], AXX, ALU.add).then_inc(r.slot, 1)

        def pool_send(eng, r, b, xn):
            eng.wait_ge(r.slot, 6 * b + 6)
            apart(eng)
            for i in range(TPB):
                for k in range(2):
                    nc.gpsimd.indirect_dma_start(
                        out=xs_dram[:, :],
                        out_offset=bass.IndirectOffsetOnAxis(
                            ap=slot[:, i, k:k + 1], axis=0),
                        in_=xn[:, i, :], in_offset=None).then_inc(r.sent, 16)

        SENT = 16 * 2 * TPB

        def pe_total(eng, r):
            eng.wait_ge(r.cum, TPB * B)
            eng.wait_ge(r.slot, 6 * B)
            nc.tensor.matmul(ps[:, 2, 0:E], ones[:], cum[:, TPB, :], start=True, stop=True).then_inc(r.total, 1)

        def dve_tables(eng, r):
            n = [0]

            def step(ins):
                ins.then_inc(r.t, 1)
                n[0] += 1
                eng.wait_ge(r.t, n[0])

            eng.wait_ge(r.total, 1)
            step(nc.vector.tensor_copy(cnt[:], ps[:, 2, 0:E]))
            step(nc.vector.tensor_tensor(padf[:], cnt[:], e_base[:], ALU.add))
            nc.vector.tensor_scalar(pad[:], padf[:], p_f[:, 0:1], None, ALU.add).then_inc(r.pad_ready, 1)
            nc.vector.memset(zrows, 0.0).then_inc(r.zero, 1)
            step(nc.vector.tensor_scalar(cnt_i[:], cnt[:], float(P - 1), None, ALU.add))
            step(nc.vector.tensor_scalar(cnt_i[:], cnt_i[:], 7, None, ALU.arith_shift_right))
            step(nc.vector.tensor_copy(nt[:], cnt_i[:]))
            step(nc.vector.tensor_tensor_scan(ends[:], nt[:], zero8[:], 0.0, ALU.add, ALU.add))
            step(nc.vector.tensor_tensor(start128[:], ends[:], nt[:], ALU.subtract))
            step(nc.vector.tensor_scalar(start128[:], start128[:], float(P), None, ALU.mult))
            step(nc.vector.tensor_tensor(abase[:], e_base[:], start128[:], ALU.subtract))
            step(nc.vector.memset(dbase[:], 0.0))
            step(nc.vector.tensor_tensor(dbase[:, 0:E - 1], abase[:, 1:E], abase[:, 0:E - 1], ALU.subtract))
            step(nc.vector.tensor_tensor(le[:], ends[:].unsqueeze(1).broadcast_to([P, TILES, E]),
                                         j_f[:].unsqueeze(2).broadcast_to([P, TILES, E]), ALU.is_le))
            step(nc.vector.tensor_reduce(ef[:], le[:], AXX, ALU.add))
            step(nc.vector.tensor_scalar(exp_tab[:], ef[:], float(E - 1), None, ALU.min))
            step(nc.vector.tensor_tensor(lep, le[:], dbase[:].unsqueeze(1).broadcast_to([P, TILES, E]), ALU.mult))
            step(nc.vector.tensor_reduce(tmpj[:], lep, AXX, ALU.add))
            step(nc.vector.scalar_tensor_tensor(rowf[:], j_f[:], float(P), tmpj[:], ALU.mult, ALU.add))
            step(nc.vector.tensor_scalar(tmpj[:], rowf[:], -1.0, float((E - 1) * REGION), ALU.mult, ALU.add))
            step(nc.vector.tensor_tensor(tmpj[:], tmpj[:], le[:, :, E - 1], ALU.mult))
            step(nc.vector.tensor_tensor(row_tab[:], rowf[:], tmpj[:], ALU.add))
            step(nc.vector.tensor_tensor(rk_y, rk[:], start128[:].unsqueeze(1).broadcast_to([P, T, E]), ALU.add))
            step(nc.vector.tensor_tensor(pick_y, oh[:], rk_y.unsqueeze(2).broadcast_to([P, T, 2, E]), ALU.mult))
            with nc.allow_low_precision(reason="row numbers below 2**24, exact in float32"):
                nc.vector.tensor_reduce(yslot[:], pick_y, AXX, ALU.add).then_inc(r.tabs, 1)
            nc.vector.memset(cum[:, 0, :], 0.0).then_inc(r.tabs, 1)
            eng.wait_ge(r.tabs, 2)

        def pool_pads(eng, r):
            eng.wait_ge(r.pad_ready, 1)
            eng.wait_ge(r.zero, 1)
            eng.wait_ge(r.sent, SENT * B)
            for e in range(E):
                nc.gpsimd.indirect_dma_start(
                    out=xs_dram[:, :], out_offset=bass.IndirectOffsetOnAxis(ap=pad[:, e:e + 1], axis=0),
                    in_=zrows, in_offset=None).then_inc(r.pad, 16)

        def expert_engines(q, r):
            STEPS = TILES + 6

            def steps(eng, body):
                for i in range(8):
                    body(i, i % 4)
                with eng.Fori(2, TILES // 4) as it:
                    for u in range(4):
                        body(it * 4 + u, u)
                for i in range(TILES, STEPS):
                    body(i, i % 4)

            def live(i, k):
                return not isinstance(i, int) or 0 <= i - k < TILES

            def ge(eng, s, v):
                if not isinstance(v, int) or v > 0:
                    eng.wait_ge(s, v)

            def turns(i, u, back):
                if isinstance(i, int):
                    return 16 * ((i - back) // 4 + 1)
                return (i - u) * 4 + 16 * ((u - back) // 4 + 1)

            def sp(eng):
                eng.wait_ge(r.tabs, 1)
                eng.wait_ge(r.pad, 16 * E)

                def body(i, u):
                    if live(i, 0):
                        ge(eng, q.tp, i - 3)
                        apart(eng)
                        row = eng.value_load(row_tab[0:1, ds(i, 1)], min_val=0, max_val=E * REGION - P)
                        eng.dma_start(xs[:, u, :], xs_dram[ds(row, P), :]).then_inc(q.ld[u], 16)
                    if live(i, 6):
                        ge(eng, q.ysb, i - 5)
                        w = (u - 6) % 4
                        apart(eng)
                        eng.dma_start(y_dram[ds((i - 6) * P, P), :], ysb[:, w, :]).then_inc(q.st[w], 16)
                steps(eng, body)
                for w in range(4):
                    eng.wait_ge(q.st[w], 16 * (TILES // 4))

            def pe(eng):
                eng.wait_ge(r.tabs, 1)
                eng.wait_ge(s_w, 32)

                def weights_of(tile):
                    return eng.value_load(exp_tab[0:1, ds(tile, 1)], min_val=0, max_val=E - 1)

                def body(i, u):
                    if live(i, 0):
                        ge(eng, q.xT, i - 1)
                        eng.wait_ge(q.ld[u], turns(i, u, 0))
                        for c in range(DC):
                            mm = nc.tensor.transpose(ps[:, u % 2, c * P:(c + 1) * P],
                                                     xs[:, u, c * P:(c + 1) * P], ident[:])
                        mm.then_inc(q.tp, 1)
                    if live(i, 1):
                        e = weights_of(i - 1)
                        w = (u + 1) % 2
                        ge(eng, q.xT, i)
                        ge(eng, q.relu, i - 2)
                        for c in range(DC):
                            mm = nc.tensor.matmul(ps[:, 2 + w, :], xsT[:, w, c * P:(c + 1) * P],
                                                  w1s[:, ds(e, 1), c:c + 1, :].rearrange("p a b f -> p (a b f)"),
                                                  start=(c == 0), stop=(c == DC - 1))
                        mm.then_inc(q.h, 1)
                    if live(i, 2):
                        w = u % 2
                        ge(eng, q.relu, i - 1)
                        ge(eng, q.hT, i - 3)
                        for c in range(FC):
                            mm = nc.tensor.transpose(ps[:, 4 + w, c * P:(c + 1) * P],
                                                     hid[:, w, c * P:(c + 1) * P], ident[:])
                        mm.then_inc(q.hTp, 1)
                    if live(i, 3):
                        e = weights_of(i - 3)
                        w = (u + 1) % 2
                        ge(eng, q.hT, i - 2)
                        ge(eng, q.ysb, i - 4)
                        for c in range(FC):
                            mm = nc.tensor.matmul(ps[:, 6 + w, 0:D], hidT[:, w, c * P:(c + 1) * P],
                                                  w2s[:, ds(e, 1), c:c + 1, :].rearrange("p a b f -> p (a b f)"),
                                                  start=(c == 0), stop=(c == FC - 1))
                        mm.then_inc(q.y, 1)
                steps(eng, body)

            def act(eng):
                def body(i, u):
                    if live(i, 0):
                        eng.wait_ge(q.tp, i + 1)
                        ge(eng, q.h, i - 1)
                        nc.scalar.copy(xsT[:, u % 2, :], ps[:, u % 2, 0:D]).then_inc(q.xT, 1)
                    if live(i, 1):
                        w = (u + 1) % 2
                        ge(eng, q.h, i)
                        ge(eng, q.hTp, i - 2)
                        nc.scalar.activation(hid[:, w, :], ps[:, 2 + w, :], ACT.Relu).then_inc(q.relu, 1)
                steps(eng, body)

            def dve(eng):
                def body(i, u):
                    if live(i, 2):
                        w = u % 2
                        ge(eng, q.hTp, i - 1)
                        ge(eng, q.y, i - 3)
                        nc.vector.tensor_copy(hidT[:, w, :], ps[:, 4 + w, :]).then_inc(q.hT, 1)
                    if live(i, 3):
                        w, v = (u + 1) % 2, (u + 1) % 4
                        ge(eng, q.y, i - 2)
                        if not isinstance(i, int) or i >= 7:
                            eng.wait_ge(q.st[v], turns(i, u, 7))
                        nc.vector.tensor_copy(ysb[:, v, :], ps[:, 6 + w, 0:D]).then_inc(q.ysb, 1)
                steps(eng, body)

            return sp, pe, act, dve

        e0, e1 = expert_engines(x0, r0), expert_engines(x1, r1)

        def pool_gather(eng, l, t, u, half):
            if not isinstance(t, int) or t >= 2:
                eng.wait_ge(s_comb[l], t - 1)
            nc.gpsimd.tensor_copy(yidx[:, u:u + 1, :], yslot[:, ds(t, 1), :]).then_inc(s_idx[l], 1)
            eng.wait_ge(s_idx[l], t + 1)
            apart(eng)
            for k in range(2):
                nc.gpsimd.indirect_dma_start(
                    out=yg[:, u, k, :], out_offset=None, in_=y_dram[:, :],
                    in_offset=bass.IndirectOffsetOnAxis(
                        ap=yidx[:, u, k:k + 1], axis=0)
                ).then_inc(s_gath[l][u], 16)

        def dve_combine(eng, l, t, u, half):
            eng.wait_ge(s_gath[l][u], half * 32 + 32)
            xt = x[:, ds(t, 1), :].rearrange("p o d -> p (o d)")
            w = wts[:, ds(t, 1), :].rearrange("p o k -> p (o k)")
            nc.vector.scalar_tensor_tensor(xt, yg[:, u, 0, :], w[:, 0:1], xt, ALU.mult, ALU.add
                                           ).then_inc(s_comb_half[l], 1)
            eng.wait_ge(s_comb_half[l], t + 1)
            nc.vector.scalar_tensor_tensor(xt, yg[:, u, 1, :], w[:, 1:2], xt, ALU.mult, ALU.add
                                           ).then_inc(s_comb[l], 1)

        def pool_prep(eng, b):
            if live_b(b, 1):
                eng.wait_ge(s_part, 128 * b)
            for i in range(TPB):
                pool_gather(eng, 0, b * TPB + i, i % 2, b * 2 + i // 2)
            pool_norm(eng, npr, b)
            eng.wait_ge(npr.xn, TPB * b + TPB)
            xb = x[:, ds(b * TPB, TPB), :]
            nc.gpsimd.tensor_tensor(xb, xb, bo[:].unsqueeze(1).broadcast_to([P, TPB, D]), ALU.add
                                    ).then_inc(s_bias, 1)

        def dve_prep(eng, b):
            for i in range(TPB):
                dve_combine(eng, 0, b * TPB + i, i % 2, b * 2 + i // 2)
            eng.wait_ge(s_comb[0], b * TPB + TPB)
            dve_norm(eng, npr, b, xn_p, (lambda: eng.wait_ge(s_part, 128 * b)) if live_b(b, 1) else None)
            dve_norm_copy(eng, npr, b)
            for c in range(2):
                for n in range(2):
                    eng.wait_ge(s_hi, 4 * b + 2 * c + n + 1)
                    nc.vector.scalar_tensor_tensor(
                        part[:, 2 * n + 1, :], ps[:, n, :], bcol[:, c, n:n + 1],
                        part[:, 2 * n, :].bitcast(F32), ALU.add, ALU.subtract).then_inc(s_lo, 1)
                for j in range(c, c + 1):
                    eng.wait_ge(s_v, 2 * b + j + 1)
                    nc.vector.tensor_tensor(
                        vs[:, vbuf(b), 2 * j:2 * j + 2, :, 0:DH],
                        ps[:, 2 + j, :].rearrange("p (i h d) -> p i h d", i=2, h=H),
                        bv[:].unsqueeze(1).broadcast_to([P, 2, H, DH]), ALU.add).then_inc(s_vs, 1)

        def act_prep(eng, b):
            act_norm(eng, npr, b)
            for c in range(2):
                for n in range(2):
                    eng.wait_ge(s_qk, 4 * b + 2 * c + n + 1)
                    if n == 0 and (c or live_b(b, 1)):
                        eng.wait_ge(s_part, 64 * (2 * b + c))
                    nc.scalar.activation(part[:, 2 * n, :], ps[:, n, :], ACT.Identity, bias=bcol[:, c, n:n + 1]
                                         ).then_inc(s_hi, 1)

        def pe_prep(eng, b):
            if live_b(b, 1):
                eng.wait_ge(s_red, 16 * (2 * b - 1))
            pe_norm(eng, npr, b, xn_p)
            eng.wait_ge(npr.ev0, b + 1)
            eng.wait_ge(npr.ev1, b + 1)
            for c in range(2):
                for n in range(2):
                    if c:
                        eng.wait_ge(s_lo, 4 * b + n + 1)
                    for k in range(DC):
                        mm = nc.tensor.matmul(ps[:, n, :], wqkv[:, k, n, P * c:P * c + P], xT[:, k, :],
                                              start=(k == 0), stop=(k == DC - 1))
                    mm.then_inc(s_qk, 1)
                for i in range(2 * c, 2 * c + 2):
                    o = ps[:, 2 + i // 2, (i % 2) * D:(i % 2) * D + D]
                    for k in range(DC):
                        mm = nc.tensor.matmul(o, xT[:, k, i * P:(i + 1) * P], wqkv[:, k, 2, :],
                                              start=(k == 0), stop=(k == DC - 1))
                mm.then_inc(s_v, 1)

        def sp_parts(eng, b, c):
            if live_b(b, 1):
                eng.wait_ge(s_ld[c], 192 * b)
                apart(eng)
            for n in range(2):
                eng.wait_ge(s_hi, 4 * b + 2 * c + n + 1)
                eng.dma_start(qk_dram[c, 2 * n], part[:, 2 * n, :].bitcast(F32)).then_inc(s_part, 16)
                eng.wait_ge(s_lo, 4 * b + 2 * c + n + 1)
                eng.dma_start(qk_dram[c, 2 * n + 1], part[:, 2 * n + 1, :].bitcast(F32)).then_inc(s_part, 16)
            eng.wait_ge(s_part, 64 * (2 * b + c + 1))

        def sp_stack(eng, b, c, u3):
            if live_b(b, 2) or (live_b(b, 1) and 2 * b + c >= 3):
                eng.wait_ge(s_sc, 32 * (2 * b + c - 2))
            rows = [(qst, 0, 0), (qst, 1, 0), (qst, 2, 1), (kst, 0, 2), (kst, 1, 3), (kst, 2, 2)]
            for dst, row, src in rows:
                for par in range(2):
                    p0 = 64 * par + DH * row
                    eng.dma_start(dst[p0:p0 + DH, u3, :, :].bitcast(F32),
                                  qk_dram[c, src].rearrange("(g r d) n -> r d g n", r=2, d=DH)[par]
                                  ).then_inc(s_ld[c], 16)

        def live_b(b, n):
            return b >= n if isinstance(b, int) else True

        def pe_max_tile(b, c, u3, s):
            pair, par, qt = s // 8, s % 2, (s % 8) // 2
            p0 = 64 * par
            return nc.tensor.matmul(ps[:, s % 4, :], qst[p0:p0 + 3 * DH, u3, pair, qt * P:(qt + 1) * P],
                                    kst[p0:p0 + 3 * DH, u3, pair, :], start=True, stop=True)

        def pe_pv(eng, b, c, m):
            g, kt = m // 4, m % 4
            U8 = 8 * (2 * b + c)
            eng.wait_ge(s_exp, 4 * (U8 + m) + 4)
            if kt == 0 and (g or c or live_b(b, 1)):
                eng.wait_ge(s_oev, 2 * (2 * b + c) + g)
            for hh in range(4):
                h = c * HU + 4 * g + hh
                mm = nc.tensor.matmul(ps[32 * hh:32 * hh + VW, O_BANK, :], vs[:, vbuf(b), kt, h, :],
                                      probs[:, (4 * m + hh) % 8, :], start=(kt == 0), stop=(kt == 3))
            mm.then_inc(s_pv, 1)

        def pe_heads(eng, n, slot_):
            eng.wait_ge(s_oev, n + 1)
            for qt in range(TPB):
                mm = nc.tensor.transpose(ps[:, T_BANK, qt * P:(qt + 1) * P], osb[:, slot_, qt * P:(qt + 1) * P],
                                         ident[:])
            mm.then_inc(s_otr, 1)

        def pe_unit(eng, b, c, nxt, last=False):
            U = None if b is None else 2 * b + c
            if nxt is not None:
                nb, ncx, nu3 = nxt
                NU = 2 * nb + ncx
                eng.wait_ge(s_ld[ncx], 192 * nb + 192)
            if b is not None:
                eng.wait_ge(s_mrow[c], 32 * b + 32)
                if c == 0:
                    eng.wait_ge(s_vs, 2 * b + 2)
            for s in range(32):
                if nxt is not None:
                    if s == 0:
                        if nxt[0] is not b:
                            if b is None:
                                eng.wait_ge(s_lo, 4)
                                eng.wait_ge(s_vs, 2)
                            elif b != 0 if isinstance(b, int) else True:
                                eng.wait_ge(r1.slot, 6 * b)
                        elif not (isinstance(b, int) and b == B - 1):
                            eng.wait_ge(s_lo, 4 * b + 8)
                            eng.wait_ge(s_vs, 2 * b + 4)
                            eng.wait_ge(s_hi, 4 * b + 8)
                    if s % 2 == 0:
                        if s >= 4:
                            eng.wait_ge(s_red, 16 * NU + s // 2 - 1)
                    mm = pe_max_tile(nb, ncx, nu3, s)
                    if s % 2 == 1:
                        mm.then_inc(s_mm, 1)
                if b is None:
                    continue
                if s >= 2 or c or live_b(b, 1):
                    eng.wait_ge(s_exp, 32 * U + s - 1)
                g, kt, hh = s // 16, (s % 16) // 4, s % 4
                pair, par = 2 * g + hh // 2, hh % 2
                p0 = 64 * par
                nc.tensor.matmul(ps[:, 4 + s % 2, :], kst[p0:p0 + 3 * DH + 1, ubuf(b, c), pair, kt * P:(kt + 1) * P],
                                 qst[p0:p0 + 3 * DH + 1, ubuf(b, c), pair, :], start=True, stop=True
                                 ).then_inc(s_sc, 1)
                if s % 4 == 3 and s >= 7:
                    pe_pv(eng, b, c, s // 4 - 1)
                if s == 9 and (c or live_b(b, 1)):
                    eng.wait_ge(s_mev, U + 1)
                    pe_heads(eng, 2 * U - 1, 1)
                if s == 25:
                    if not (c or live_b(b, 1)):
                        eng.wait_ge(s_mev, U + 1)
                    else:
                        eng.wait_ge(s_at, 2 * U)
                    pe_heads(eng, 2 * U, 0)
            if b is not None:
                pe_pv(eng, b, c, 7)
            if nxt is not None:
                if b is not None:
                    eng.wait_ge(s_at, 2 * U + 1)
                eng.wait_ge(s_red, 16 * NU + 16)
                nc.tensor.transpose(ps[0:32, T_BANK, 0:P], mx[:], ident[:]).then_inc(s_mtr, 1)
            if last:
                eng.wait_ge(s_at, 2 * U + 1)
                pe_heads(eng, 2 * U + 1, 1)

        def act_unit(eng, b, c, nxt, last=False):
            U = None if b is None else 2 * b + c

            def heads_copy(g):
                eng.wait_ge(s_pv, 8 * U + 4 * g + 4)
                if g or c or live_b(b, 1):
                    if 2 * 0 + g or c or live_b(b, 1):
                        pass
                if not (isinstance(U, int) and 2 * U + g < 2):
                    eng.wait_ge(s_otr, 2 * U + g - 1)
                nc.scalar.copy(osb[:, g, :], ps[:, O_BANK, :]).then_inc(s_oev, 1)

            if b is not None:
                for s in range(32):
                    eng.wait_ge(s_sc, 32 * U + s + 1)
                    if s >= 8 or c or live_b(b, 1):
                        eng.wait_ge(s_pv, 8 * U + s // 4 - 1)
                    nc.scalar.activation(probs[:, s % 8, :], ps[:, 4 + s % 2, :], ACT.Exp, scale=LOGIT_SCALE
                                         ).then_inc(s_exp, 1)
                    if s == 21:
                        heads_copy(0)
                heads_copy(1)
            if nxt is not None:
                nb, ncx, nu3 = nxt
                NU = 2 * nb + ncx
                eng.wait_ge(s_mtr, NU + 1)
                if live_b(nb, 1) or ncx:
                    if ncx:
                        eng.wait_ge(s_mrow[0], 32 * nb + 32)
                    else:
                        eng.wait_ge(s_mrow[1], 32 * nb)
                nc.scalar.activation(mT[:], ps[0:32, T_BANK, 0:P], ACT.Copy, scale=-1.0).then_inc(s_mev, 1)
                eng.wait_ge(s_mev, NU + 1)
                for par in range(2):
                    r = 64 * par + 3 * DH
                    eng.dma_start(qst[r:r + 1, nu3, :, :].bitcast(F32), mT[16 * par:16 * par + 16, :].bitcast(F32)
                                  ).then_inc(s_mrow[ncx], 16)

        def dve_unit(eng, b, c, nxt, last=False):
            U = None if b is None else 2 * b + c

            def normalise(n, u3, g, src):
                eng.wait_ge(s_otr, n + 1)
                o = ps[:, T_BANK, :].rearrange("p (q h w) -> p q h w", q=TPB, h=4)
                if not (isinstance(n, int) and n == 0):
                    eng.wait_ge(s_at, n)
                nc.vector.reciprocal(rs[:].unsqueeze(3), o[:, :, :, DH:DH + 1]).then_inc(s_rec, 1)
                eng.wait_ge(s_rec, n + 1)
                dst = attn[:, u3, :, 64 * g:64 * g + 64].rearrange("p q (h d) -> p q h d", h=4)
                nc.vector.tensor_tensor(dst, o[:, :, :, 0:DH], rs[:].unsqueeze(3).broadcast_to([P, TPB, 4, DH]),
                                        ALU.mult).then_inc(s_at, 1)

            for j in range(16):
                if nxt is not None:
                    nb, ncx, nu3 = nxt
                    NU = 2 * nb + ncx
                    if j == 0 and (ncx or live_b(nb, 1)):
                        eng.wait_ge(s_mtr, NU)
                    eng.wait_ge(s_mm, 16 * NU + j + 1)
                    col = j
                    dst = mx[:].rearrange("p (r c) -> p r c", r=2)[:, :, col:col + 1]
                    bk = (2 * j) % 4
                    nc.vector.tensor_reduce(dst, ps[:, bk:bk + 2, :].unsqueeze(2), AXX, ALU.max
                                            ).then_inc(s_red, 1)
                if b is None:
                    continue
                if j == 5 and (c or live_b(b, 1)):
                    normalise(2 * U - 1, ubuf_prev(b, c), 1, 1)
                if j == 13:
                    normalise(2 * U, ubuf(b, c), 0, 0)
            if last:
                normalise(2 * U + 1, ubuf(b, c), 1, 1)

        def pe_post(eng, b, nu):
            eng.wait_ge(s_red, 16 * nu)
            eng.wait_ge(s_at, 4 * b + 4)
            for c in range(DC):
                for qt in range(TPB):
                    mm = nc.tensor.transpose(ps[:, c, qt * P:(qt + 1) * P], attn[:, ubuf(b, c), qt, :], ident[:])
                mm.then_inc(s_ptr, 1)
            eng.wait_ge(s_pev0, b + 1)
            eng.wait_ge(s_pev1, b + 1)
            for i in range(TPB):
                o = ps[:, 2 + i // 2, (i % 2) * D:(i % 2) * D + D]
                for k in range(DC):
                    mm = nc.tensor.matmul(o, xT[:, k, i * P:(i + 1) * P], wout[:, k, :],
                                          start=(k == 0), stop=(k == DC - 1))
                if i % 2:
                    mm.then_inc(s_prj, 1)
            pe_norm(eng, r1.norm, b, xn_r)
            pe_route(eng, r1, b, xn_r)

        def act_post(eng, b, np_):
            eng.wait_ge(s_ptr, 2 * b + 1)
            nc.scalar.copy(xT[:, 0, :], ps[:, 0, :]).then_inc(s_pev0, 1)
            eng.wait_ge(s_prj, 2 * b + 2)
            act_norm(eng, r1.norm, b)
            act_route(eng, r1, b)

        def dve_post(eng, b, np_):
            eng.wait_ge(s_ptr, 2 * b + 2)
            nc.vector.tensor_copy(xT[:, 1, :], ps[:, 1, :]).then_inc(s_pev1, 1)
            eng.wait_ge(s_bias, b + 1)
            for j in range(2):
                eng.wait_ge(s_prj, 2 * b + j + 1)
                xb = x[:, ds(b * TPB + 2 * j, 2), :]
                nc.vector.tensor_tensor(xb, ps[:, 2 + j, :].rearrange("p (i d) -> p i d", i=2), xb, ALU.add
                                        ).then_inc(s_x2, 1)
            eng.wait_ge(s_x2, 2 * b + 2)
            dve_norm(eng, r1.norm, b, xn_r, (lambda: eng.wait_ge(r1.free, b + 1)) if live_b(b, 1) else None)
            dve_norm_copy(eng, r1.norm, b)
            dve_route(eng, r1, b)

        def pool_post(eng, b):
            pool_norm(eng, r1.norm, b)
            pool_send(eng, r1, b, xn_r)
            eng.wait_ge(r1.sent, SENT * b + SENT)
            eng.sem_inc(r1.free, 1)

        class Batch:
            pass

        mod3 = {}

        def vbuf(b):
            return b % 3 if isinstance(b, int) else mod3[id(b)]

        def ubuf(b, c):
            return (2 * vbuf(b) + c) % 3

        def ubuf_prev(b, c):
            return (ubuf(b, c) - 1) % 3

        raise_if = None

        def attention(eng, unit, prep, post, parts=None):
            def batch(b, b1, bm, first=False, last=False):
                if not last:
                    prep(b1, b, True)
                unit(b, 0, (b, 1, ubuf(b, 1)), False)
                if not first:
                    post(bm, 2 * b + 2, b if last else b1)
                if not last:
                    prep(b1, b, False)
                unit(b, 1, None if last else (b1, 0, ubuf(b1, 0)), last)

            prep(0, None, True)
            prep(0, None, False)
            unit(None, 0, (0, 0, ubuf(0, 0)), False)
            batch(0, 1, None, first=True)
            with eng.Fori(0, (B - 2) // 3) as it:
                for j in range(3):
                    vals = [it * 3 + (1 + j + d) if 1 + j + d else it * 3 for d in (0, 1, -1)]
                    for v, d in zip(vals, (0, 1, -1)):
                        mod3[id(v)] = (1 + j + d) % 3
                    keep.append(vals)
                    batch(*vals)
            batch(B - 1, None, B - 2, last=True)
            post(B - 1, 2 * B, B)

        keep = []

        @block.sync
        def _(eng):
            with eng.Fori(0, B) as g:
                eng.dma_start(x[:, ds(g * TPB, TPB), :], x_tok[:, ds(g * TPB, TPB), :]).then_inc(s_x, 16)
                eng.wait_ge(s_x, g * 16 + 16)
                apart(eng)
            e0[0](eng)

            def prep(b, bb, early):
                if early:
                    sp_parts(eng, b, 0)
                    sp_stack(eng, b, 0, ubuf(b, 0))
                    sp_parts(eng, b, 1)
                else:
                    sp_stack(eng, b, 1, ubuf(b, 1))
            attention(eng, lambda *a: None, prep, lambda *a: None)
            e1[0](eng)
            with eng.Fori(0, T) as t:
                eng.wait_ge(s_comb[1], t + 1)
                apart(eng)
                eng.dma_start(out_tok[:, ds(t, 1), :], x[:, ds(t, 1), :]).then_inc(s_out, 16)
            eng.wait_ge(s_out, 16 * T)

        @block.gpsimd
        def _(eng):
            nc.gpsimd.iota(e_i[:], pattern=[[1, E]], base=0, channel_multiplier=0).then_inc(s_iota, 1)
            nc.gpsimd.iota(p_i[:], pattern=[[0, 1]], base=0, channel_multiplier=1).then_inc(s_iota, 1)
            nc.gpsimd.iota(j_i[:], pattern=[[1, TILES]], base=0, channel_multiplier=0).then_inc(s_iota, 1)
            nc.gpsimd.memset(ident[:], 0.0).then_inc(s_iota, 1)
            nc.gpsimd.memset(ones[:], 1.0).then_inc(s_iota, 1)
            nc.gpsimd.memset(mhalf[:], -0.5).then_inc(s_const, 1)
            eng.sem_inc(r1.free, 1)
            nc.gpsimd.memset(vs[:], 1.0).then_inc(s_const, 1)
            eng.wait_ge(s_iota, 5)
            nc.gpsimd.affine_select(out=ident[:], in_=ident[:], compare_op=ALU.not_equal, fill=1.0, base=0,
                                    pattern=[[-1, P]], channel_multiplier=1).then_inc(s_const, 1)
            nc.gpsimd.affine_select(out=upper[:], in_=ones[:], compare_op=ALU.is_gt, fill=0.0, base=0,
                                    pattern=[[1, P]], channel_multiplier=-1).then_inc(s_const, 1)
            eng.wait_ge(s_const, 4)
            eng.wait_ge(s_small, 16 * 37)
            for c in range(DC):
                for n in range(3):
                    nc.gpsimd.tensor_copy(
                        wqkv[:, c, n, :].rearrange("p (h d) -> p h d", h=H),
                        wraw[:, c, :].rearrange("p (h n d) -> p n h d", n=3, d=DH)[:, n]).then_inc(s_sorted, 1)
            pool_norm(eng, r0.norm, 0)
            with eng.Fori(1, B) as g:
                pool_norm(eng, r0.norm, g)
                pool_send(eng, r0, g - 1, xn_r)
            pool_send(eng, r0, B - 1, xn_r)
            pool_pads(eng, r0)
            for w in range(4):
                eng.wait_ge(x0.st[w], 16 * (TILES // 4))

            def prep(b, bb, early):
                if early:
                    pool_prep(eng, b)
            attention(eng, lambda *a: None, prep, lambda b, nu, np_: pool_post(eng, b))
            pool_pads(eng, r1)
            for w in range(4):
                eng.wait_ge(x1.st[w], 16 * (TILES // 4))
            for t in range(2):
                pool_gather(eng, 1, t, t, 0)
            with eng.Fori(1, T // 2) as it:
                for u in range(2):
                    pool_gather(eng, 1, it * 2 + u, u, it)

        @block.scalar
        def _(eng):
            with nc.allow_non_contiguous_dma(reason="bias columns"):
                eng.dma_start(wg[:], w_gate.rearrange("(c p) e -> p c e", p=P)).then_inc(s_small, 16)
                eng.dma_start(wraw,
                              w_qkv.rearrange("(c p) n -> p c n", p=P)).then_inc(s_small, 16)
                eng.dma_start(wout[:], w_out.rearrange("(c p) n -> p c n", p=P)).then_inc(s_small, 16)
                bq = b_qkv.rearrange("(c h n d) -> n c h d", c=2, n=3, d=DH)
                for n in range(2):
                    for c in range(2):
                        for h in range(HU):
                            eng.dma_start(bcol[DH * h:DH * h + DH, c, n:n + 1],
                                          bq[n, c, h].unsqueeze(1)).then_inc(s_small, 16)
                eng.dma_start(bv[:], b_qkv.rearrange("(o h n d) -> n o h d", o=1, n=3, d=DH)[2]
                              .broadcast_to([P, H, DH])).then_inc(s_small, 16)
                eng.dma_start(bo[:], b_out.rearrange("(o d) -> o d", o=1).broadcast_to([P, D])
                              ).then_inc(s_small, 16)
            eng.dma_start(w1s[:], w1.rearrange("e (c p) f -> p e c f", p=P)).then_inc(s_w, 16)
            eng.dma_start(w2s[:], w2.rearrange("e (c p) f -> p e c f", p=P)).then_inc(s_w, 16)

            def route0(g):
                act_norm(eng, r0.norm, g)
                act_route(eng, r0, g)
            route0(0)
            with eng.Fori(1, B) as g:
                route0(g)
            e0[2](eng)

            def prep(b, bb, early):
                if early:
                    act_prep(eng, b)
            attention(eng, lambda *a: act_unit(eng, *a), prep, lambda b, nu, np_: act_post(eng, b, np_))
            e1[2](eng)

        @block.tensor
        def _(eng):
            eng.wait_ge(s_const, 4)
            eng.wait_ge(s_dve0, NCONST)
            eng.wait_ge(s_small, 16 * 37)

            def route0(g):
                if live_b(g, 1):
                    eng.wait_ge(r0.slot, 6 * g)
                pe_norm(eng, r0.norm, g, xn_r)
                pe_route(eng, r0, g, xn_r)
            route0(0)
            with eng.Fori(1, B) as g:
                route0(g)
            pe_total(eng, r0)
            e0[1](eng)
            eng.wait_ge(s_sorted, 3 * DC)
            eng.wait_ge(x0.ysb, TILES)
            for done in (x0.xT, x0.relu, x0.hT):
                eng.wait_ge(done, TILES)
            eng.wait_ge(s_dve0, NCONST + 1)

            def prep(b, bb, early):
                if early:
                    pe_prep(eng, b)
            attention(eng, lambda *a: pe_unit(eng, *a), prep, lambda b, nu, np_: pe_post(eng, b, nu))
            pe_total(eng, r1)
            e1[1](eng)

        @block.vector
        def _(eng):
            eng.wait_ge(s_iota, 3)
            nc.vector.tensor_copy(e_f[:], e_i[:]).then_inc(s_dve0, 1)
            nc.vector.tensor_copy(p_f[:], p_i[:]).then_inc(s_dve0, 1)
            nc.vector.tensor_copy(j_f[:], j_i[:]).then_inc(s_dve0, 1)
            nc.vector.memset(zero8[:], 0.0).then_inc(s_dve0, 1)
            nc.vector.memset(cum[:, 0, :], 0.0).then_inc(s_dve0, 1)
            nc.vector.memset(kst[:].bitcast(F32), 1.0).then_inc(s_dve0, 1)
            nc.vector.memset(ps[:, O_BANK, :], 0.0).then_inc(s_dve0, 1)
            eng.wait_ge(s_dve0, 1)
            nc.vector.tensor_scalar(e_base[:], e_f[:], float(REGION), None, ALU.mult).then_inc(s_dve0, 1)
            eng.wait_ge(s_dve0, NCONST)

            def route0(g):
                eng.wait_ge(s_x, g * 16 + 16)
                dve_norm(eng, r0.norm, g, xn_r,
                         (lambda: eng.wait_ge(r0.sent, SENT * g)) if live_b(g, 1) else None)
                dve_norm_copy(eng, r0.norm, g)
                dve_route(eng, r0, g)
            route0(0)
            with eng.Fori(1, B) as g:
                route0(g)
            eng.wait_ge(s_sorted, 3 * DC)
            dve_tables(eng, r0)
            e0[3](eng)
            eng.wait_ge(x0.ysb, TILES)
            nc.vector.memset(ps[:, O_BANK, :], 0.0).then_inc(s_dve0, 1)
            eng.wait_ge(s_small, 16 * 37)

            def prep(b, bb, early):
                if early:
                    dve_prep(eng, b)
            attention(eng, lambda *a: dve_unit(eng, *a), prep, lambda b, nu, np_: dve_post(eng, b, np_))
            dve_tables(eng, r1)
            e1[3](eng)
            for t in range(2):
                dve_combine(eng, 1, t, t, 0)
            with eng.Fori(1, T // 2) as it:
                for u in range(2):
                    dve_combine(eng, 1, it * 2 + u, u, it)


_INS = ['L0_attn_X', 'L0_attn_W_qkv', 'L0_attn_b_qkv', 'L0_attn_W_out', 'L0_attn_b_out',
        'L0_ffn_Wg', 'L0_ffn_W1', 'L0_ffn_W2']


def kernel(**inputs):
    import concourse.bacc as bacc
    from concourse.bass_utils import run_bass_kernel_spmd

    nc = bacc.Bacc("TRN2", target_bir_lowering=False, num_devices=1, dynamic_dma_scratch_size=4096)
    arrays, args = {}, []
    for name in _INS:
        a = np.ascontiguousarray(inputs[name])
        arrays[f"in_{name}"] = a
        args.append(nc.dram_tensor(f"in_{name}", a.shape, mybir.dt.from_np(a.dtype), kind="ExternalInput").ap())
    shape = inputs['L0_attn_X'].shape
    args.append(nc.dram_tensor("out_0", shape, F32, kind="ExternalOutput").ap())
    macaron_kernel(nc, *args)
    r = run_bass_kernel_spmd(nc, [arrays], core_ids=[0])
    return r.results[0]["out_0"]
```

```python
from contextlib import ExitStack

import numpy as np
import concourse.bass as bass
from concourse import mybir

P = 128
F32 = mybir.dt.float32
F32R = mybir.dt.float32r
U32 = mybir.dt.uint32
I32 = mybir.dt.int32
ACT = mybir.ActivationFunctionType
ALU = mybir.AluOpType
AXX = mybir.AxisListType.X
ds = bass.ds


def macaron_kernel(nc, x_in, w_qkv, b_qkv, w_out, b_out, w_gate, w1, w2, out):
    B, S, D = x_in.shape
    E, _, F = w1.shape
    H = 16
    DH = D // H
    TPB = S // P
    T = B * TPB
    DC = D // P
    FC = F // P
    G4 = TPB * E
    REGION = T * P + P
    TILES = -(-(2 * T + E - 1) // 4) * 4
    HU = H // 2
    PAIRS = HU // 2
    VW = DH + 1
    LOGIT_SCALE = 1.0 / float(np.sqrt(DH))
    assert S == 512 and D == 256 and E == 8 and TPB == 4

    x_tok = x_in.rearrange("b (i p) d -> p (b i) d", p=P)
    out_tok = out.rearrange("b (i p) d -> p (b i) d", p=P)

    xs_dram = nc.dram_tensor("xs_lists", [E * REGION, D], F32, kind="Internal").ap()
    y_dram = nc.dram_tensor("y_tiles", [TILES * P, D], F32, kind="Internal").ap()
    qk_dram = nc.dram_tensor("qk_parts", [2, 4, P, S], F32, kind="Internal").ap()

    with ExitStack() as ctx:
        def sb(name, shape, dt=F32):
            return ctx.enter_context(nc.sbuf_tensor(name, shape, dt))

        def sem(name):
            return ctx.enter_context(nc.semaphore(name))

        x = sb("x", [P, T, D])
        w1s = sb("w1s", [P, E, DC, F])
        w2s = sb("w2s", [P, E, FC, D])
        kst = sb("kst", [P, 4, PAIRS, S], F32R)
        qst = sb("qst", [P, 4, PAIRS, S], F32R)
        probs = w2s[:].rearrange("p e c d -> p (e c d)").rearrange("p (r s) -> p r s", s=S)
        vs = sb("vs", [P, 2, TPB, H, VW])
        osb = sb("osb", [P, 2, S])
        attn = sb("attn", [P, 4, TPB, P])
        xT = sb("xT", [P, DC, S])
        wqkv = sb("wqkv", [P, DC, 3, D])
        wout = sb("wout", [P, DC, D])
        wg = sb("wg", [P, DC, E])
        part = sb("part", [P, 4, S], F32R)
        bcol = sb("bcol", [P, 2, 2])
        bv = sb("bv", [P, H, DH])
        bo = sb("bo", [P, D])
        ident = sb("ident", [P, P])
        ones = sb("ones", [P, P])
        upper = sb("upper", [P, P])
        xn_r = sb("xn_r", [P, TPB, D])
        mx = sb("mx", [P, 32])
        mT = sb("mT", [32, P], F32R)
        rs = sb("rs", [P, TPB, 4])
        flat = part[:].bitcast(F32).rearrange("p n s -> p (n s)")
        xn_p = flat[:, 0:TPB * D].rearrange("p (i d) -> p i d", d=D)
        yg = flat[:, TPB * D:2 * TPB * D].rearrange("p (u k d) -> p u k d", u=2, k=2)
        osb_flat = osb[:].rearrange("p n s -> p (n s)")
        xs = flat[:, 0:4 * D].rearrange("p (r d) -> p r d", r=4)
        hid = flat[:, 4 * D:4 * D + 2 * F].rearrange("p (r d) -> p r d", r=2)
        hidT = osb_flat[:, 0:2 * F].rearrange("p (r d) -> p r d", r=2)
        xsT = xT[:].rearrange("p c s -> p (c s)")[:, 0:2 * D].rearrange("p (r d) -> p r d", r=2)
        ysb = attn[:].rearrange("p a q n -> p (a q n)")[:, 0:4 * D].rearrange("p (r d) -> p r d", r=4)
        stats = sb("stats", [P, TPB, 6])
        mv = sb("mv", [P, TPB, 2])
        veps = sb("veps", [P, TPB])
        mhalf = sb("mhalf", [P, TPB])
        rstd = sb("rstd", [P, TPB])
        nmr = sb("nmr", [P, TPB])
        lg = sb("lg", [P, TPB, E])
        m8 = sb("m8", [P, TPB, 8])
        i8 = sb("i8", [P, TPB, 8], U32)
        i8f = sb("i8f", [P, TPB, 2])
        gap = sb("gap", [P, TPB])
        gexp = sb("gexp", [P, TPB])
        gden = sb("gden", [P, TPB])
        grec = sb("grec", [P, TPB])
        wts = sb("wts", [P, T, 2])
        oh = sb("oh", [P, T, 2, E])
        both = sb("both", [P, TPB, E])
        cum = sb("cum", [P, TPB + 1, E])
        rk = sb("rk", [P, T, E])
        rk_base = sb("rk_base", [P, TPB, E])
        pick = sb("pick", [P, TPB, 2, E])
        slot = sb("slot", [P, TPB, 2], U32)
        e_i = sb("e_i", [P, E], I32)
        e_f = sb("e_f", [P, E])
        e_base = sb("e_base", [P, E])
        p_i = sb("p_i", [P, 1], I32)
        p_f = sb("p_f", [P, 1])
        j_f = sb("j_f", [P, TILES])
        cnt = sb("cnt", [P, E])
        cnt_i = sb("cnt_i", [P, E], I32)
        nt = sb("nt", [P, E])
        zero8 = sb("zero8", [P, E])
        ends = sb("ends", [P, E])
        start128 = sb("start128", [P, E])
        abase = sb("abase", [P, E])
        dbase = sb("dbase", [P, E])
        padf = sb("padf", [P, E])
        pad = sb("pad", [P, E], U32)
        exp_tab = sb("exp_tab", [P, TILES], I32)
        row_tab = sb("row_tab", [P, TILES], I32)
        yslot = sb("yslot", [P, T, 2], U32)
        yidx = sb("yidx", [P, 2, 2], U32)

        ps = ctx.enter_context(nc.psum_tensor("ps", [P, 8, 512], F32))
        O_BANK, T_BANK = 6, 7

        def room(at, n):
            return flat[:, at:at + n]

        zrows = room(0, D)
        rk_y = room(D, T * E).rearrange("p (t e) -> p t e", e=E)
        pick_y = room(2 * D, 2 * T * E).rearrange("p (t k e) -> p t k e", k=2, e=E)
        le = room(4 * D, TILES * E).rearrange("p (j e) -> p j e", e=E)
        lep = osb_flat[:, 0:TILES * E].rearrange("p (j e) -> p j e", e=E)
        ef, rowf, tmpj, j_scratch = (room(4 * D + TILES * (E + n), TILES) for n in range(4))
        j_i = j_scratch.bitcast(I32)
        wraw = vs[:].rearrange("p u t h w -> p (u t h w)")[:, 0:DC * 3 * D].rearrange("p (c n) -> p c n", c=DC)

        s_x = sem("x_loaded")
        s_w = sem("ffn_weights_loaded")
        s_wg = sem("gate_weights_loaded")
        s_small = sem("small_weights_loaded")
        s_sorted = sem("qkv_columns_sorted")
        s_iota = sem("iotas_made")
        s_const = sem("constants_made")
        s_dve0 = sem("dve_constants_made")

        class Norm:

            def __init__(self, n):
                self.stats = sem(n + "_stats")
                self.mv = sem(n + "_mean_var")
                self.veps = sem(n + "_var_eps")
                self.rstd = sem(n + "_rstd")
                self.nmr = sem(n + "_neg_mean_rstd")
                self.xn = sem(n + "_rows")
                self.tp = sem(n + "_transposed")
                self.ev0 = sem(n + "_chunk0_copied")
                self.ev1 = sem(n + "_chunk1_copied")

        class Route:

            def __init__(self, n, at):
                self.norm = Norm(n)
                self.lg_at, self.rank_at = at
                self.lg = sem(n + "_logits")
                self.d = sem(n + "_dve_step")
                self.gap = sem(n + "_gap_ready")
                self.exp = sem(n + "_gap_exp")
                self.cum = sem(n + "_counts_ready")
                self.rank = sem(n + "_ranks")
                self.slot = sem(n + "_slots")
                self.sent = sem(n + "_rows_sent")
                self.free = sem(n + "_rows_free")
                self.total = sem(n + "_totals")
                self.t = sem(n + "_table_step")
                self.tabs = sem(n + "_tables_ready")
                self.zero = sem(n + "_zero_rows")
                self.pad = sem(n + "_pads_sent")
                self.pad_ready = sem(n + "_pad_rows_ready")

        class Expert:

            def __init__(self, n):
                self.ld = [sem(f"{n}_rows_loaded{r}") for r in range(4)]
                self.tp = sem(n + "_rows_transposed")
                self.xT = sem(n + "_rowsT_copied")
                self.h = sem(n + "_hidden_made")
                self.relu = sem(n + "_hidden_relu")
                self.hTp = sem(n + "_hidden_transposed")
                self.hT = sem(n + "_hiddenT_copied")
                self.y = sem(n + "_y_made")
                self.ysb = sem(n + "_y_copied")
                self.st = [sem(f"{n}_y_stored{r}") for r in range(4)]

        r0 = Route("r0", at=((2, 0), (3, 0)))
        r1 = Route("r1", at=((7, 0), (7, 64)))
        npr = Norm("pr")
        x0, x1 = Expert("x0"), Expert("x1")
        s_gath = [[sem(f"gathered{l}_{r}") for r in range(2)] for l in range(2)]
        s_idx = [sem(f"gather_rows{l}") for l in range(2)]
        s_comb = [sem(f"combined{l}") for l in range(2)]
        s_comb_half = [sem(f"combined_half{l}") for l in range(2)]
        s_qk = sem("qk_products")
        s_hi = sem("qk_hi")
        s_lo = sem("qk_lo")
        s_v = sem("v_products")
        s_vs = sem("v_copied")
        s_part = sem("parts_stored")
        s_ld = [sem(f"stack_loaded{c}") for c in range(2)]
        s_bias = sem("out_bias_added")
        s_mm = sem("max_scores")
        s_red = sem("max_reduced")
        s_mtr = sem("max_transposed")
        s_mev = sem("max_negated")
        s_mrow = [sem(f"max_row_placed{c}") for c in range(2)]
        s_sc = sem("scores")
        s_exp = sem("exps")
        s_pv = sem("pv")
        s_oev = sem("heads_copied")
        s_otr = sem("heads_transposed")
        s_rec = sem("sums_inverted")
        s_at = sem("heads_normalised")
        s_ptr = sem("attn_transposed")
        s_pev0 = sem("attnT0_copied")
        s_pev1 = sem("attnT1_copied")
        s_prj = sem("projected")
        s_x2 = sem("attention_added")
        s_out = sem("out_stored")

        NCONST = 8
        SMALL = 16 * (2 + 4 * HU + 2)

        block = ctx.enter_context(nc.Block())

        def apart(eng):
            eng.nop(nofuse=True)

        def batch_rows(b, i=0, n=1):
            return x[:, ds(b * TPB + i, n), :]

        def dve_stats(eng, n, b):
            apart(eng)
            for i in range(TPB):
                nc.vector.bn_stats(stats[:, i, :], x[:, ds(b * TPB + i, 1), :].rearrange("p o d -> p (o d)")
                                   ).then_inc(n.stats, 1)
            eng.wait_ge(n.stats, TPB * b + TPB)
            apart(eng)
            for i in range(TPB):
                nc.vector.bn_aggr(mv[:, i, :], stats[:, i, :]).then_inc(n.mv, 1)
            eng.wait_ge(n.mv, TPB * b + TPB)
            nc.vector.tensor_scalar(veps[:], mv[:, :, 1], 1e-5, None, ALU.add).then_inc(n.veps, 1)

        def dve_rows(eng, n, b, xn, xn_free=None):
            eng.wait_ge(n.rstd, b + 1)
            nc.vector.scalar_tensor_tensor(nmr[:], mv[:, :, 0], -1.0, rstd[:], ALU.mult, ALU.mult
                                           ).then_inc(n.nmr, 1)
            if xn_free is not None:
                xn_free()
            eng.wait_ge(n.nmr, b + 1)
            for i in range(TPB):
                nc.vector.tensor_scalar(xn[:, i, :], x[:, ds(b * TPB + i, 1), :].rearrange("p o d -> p (o d)"),
                                        rstd[:, i:i + 1], nmr[:, i:i + 1], ALU.mult, ALU.add
                                        ).then_inc(n.xn, 1)

        def dve_norm(eng, n, b, xn, xn_free=None):
            dve_stats(eng, n, b)
            dve_rows(eng, n, b, xn, xn_free)

        def pool_norm(eng, n, b):
            eng.wait_ge(n.veps, b + 1)
            nc.gpsimd.tensor_tensor(rstd[:], veps[:], mhalf[:], ALU.pow).then_inc(n.rstd, 1)

        def pe_norm(eng, n, b, xn, chunks=range(DC), banks=(0, 1)):
            eng.wait_ge(n.xn, TPB * b + TPB)
            for c in chunks:
                for i in range(TPB):
                    mm = nc.tensor.transpose(ps[:, banks[c], i * P:(i + 1) * P], xn[:, i, c * P:(c + 1) * P],
                                             ident[:])
                mm.then_inc(n.tp, 1)

        def act_norm(eng, n, b, bank=0):
            eng.wait_ge(n.tp, 2 * b + 1)
            nc.scalar.copy(xT[:, 0, :], ps[:, bank, :]).then_inc(n.ev0, 1)

        def dve_norm_copy(eng, n, b, bank=1):
            eng.wait_ge(n.tp, 2 * b + 2)
            nc.vector.tensor_copy(xT[:, 1, :], ps[:, bank, :]).then_inc(n.ev1, 1)

        def pe_logits(eng, r, b):
            eng.wait_ge(r.norm.ev0, b + 1)
            eng.wait_ge(r.norm.ev1, b + 1)
            bank, at = r.lg_at
            for i in range(TPB):
                for c in range(DC):
                    mm = nc.tensor.matmul(ps[:, bank, at + i * E:at + (i + 1) * E], xT[:, c, i * P:(i + 1) * P], wg[:, c, :],
                                          start=(c == 0), stop=(c == DC - 1))
            mm.then_inc(r.lg, 1)

        def pe_ranks(eng, r, b):
            eng.wait_ge(r.cum, TPB * b + TPB)
            bank, at = r.rank_at
            nc.tensor.matmul(ps[:, bank, at:at + G4], upper[:], both[:].rearrange("p i e -> p (i e)"),
                             start=True, stop=False)
            nc.tensor.matmul(ps[:, bank, at:at + G4], ones[:], cum[:, 0:TPB, :].rearrange("p i e -> p (i e)"),
                             start=False, stop=True).then_inc(r.rank, 1)

        def act_route(eng, r, b):
            eng.wait_ge(r.gap, b + 1)
            nc.scalar.activation(gexp[:], gap[:], ACT.Exp).then_inc(r.exp, 1)

        NSTEP = 2 * TPB + 6

        def dve_top2(eng, r, b):
            eng.wait_ge(r.lg, b + 1)
            base = NSTEP * b
            bank, at = r.lg_at
            nc.vector.tensor_copy(lg[:], ps[:, bank, at:at + G4].rearrange("p (i e) -> p i e", e=E)).then_inc(r.d, 1)
            eng.wait_ge(r.d, base + 1)
            apart(eng)
            for i in range(TPB):
                nc.vector.max(m8[:, i, :], lg[:, i, :]).then_inc(r.d, 1)
            eng.wait_ge(r.d, base + 1 + TPB)
            apart(eng)
            for i in range(TPB):
                nc.vector.max_index(i8[:, i, :], m8[:, i, :], lg[:, i, :]).then_inc(r.d, 1)
            nc.vector.tensor_tensor(gap[:], m8[:, :, 1], m8[:, :, 0], ALU.subtract).then_inc(r.gap, 1)

        def dve_onehots(eng, r, b):
            base = NSTEP * b
            eng.wait_ge(r.d, base + 1 + 2 * TPB)
            nc.vector.tensor_copy(i8f[:], i8[:, :, 0:2]).then_inc(r.d, 1)
            eng.wait_ge(r.d, base + 2 + 2 * TPB)
            ohb = oh[:, ds(b * TPB, TPB), :, :]
            nc.vector.tensor_tensor(
                ohb, i8f[:].unsqueeze(3).broadcast_to([P, TPB, 2, E]),
                e_f[:].unsqueeze(1).unsqueeze(1).broadcast_to([P, TPB, 2, E]), ALU.is_equal).then_inc(r.d, 1)
            eng.wait_ge(r.d, base + 3 + 2 * TPB)
            ohb0 = oh[:, ds(b * TPB, TPB), 0:1, :].rearrange("p i o e -> p i (o e)")
            ohb1 = oh[:, ds(b * TPB, TPB), 1:2, :].rearrange("p i o e -> p i (o e)")
            nc.vector.tensor_tensor(both[:], ohb0, ohb1, ALU.add).then_inc(r.d, 1)

        def dve_counts(eng, r, b):
            base = NSTEP * b
            eng.wait_ge(r.d, base + 4 + 2 * TPB)
            for i in range(TPB):
                nc.vector.tensor_tensor(cum[:, i + 1, :], cum[:, i, :], both[:, i, :], ALU.add).then_inc(r.cum, 1)
                eng.wait_ge(r.cum, TPB * b + i + 1)

        def dve_weights(eng, r, b):
            base = NSTEP * b
            eng.wait_ge(r.exp, b + 1)
            nc.vector.tensor_scalar(gden[:], gexp[:], 2.0, 2.0, ALU.mult, ALU.add).then_inc(r.d, 1)
            eng.wait_ge(r.d, base + 5 + 2 * TPB)
            nc.vector.reciprocal(grec[:], gden[:]).then_inc(r.d, 1)
            eng.wait_ge(r.d, base + 6 + 2 * TPB)
            apart(eng)
            nc.vector.tensor_copy(wts[:, ds(b * TPB, TPB), 0:1], grec[:].unsqueeze(2))
            nc.vector.tensor_tensor(wts[:, ds(b * TPB, TPB), 1:2], grec[:].unsqueeze(2), gexp[:].unsqueeze(2),
                                    ALU.mult).then_inc(r.slot, 1)

        def dve_slots(eng, r, b):
            ohb = oh[:, ds(b * TPB, TPB), :, :]
            eng.wait_ge(r.rank, b + 1)
            apart(eng)
            bank, at = r.rank_at
            rkv = ps[:, bank, at:at + G4].rearrange("p (i e) -> p i e", e=E)
            nc.vector.tensor_copy(rk[:, ds(b * TPB, TPB), :], rkv).then_inc(r.slot, 1)
            nc.vector.tensor_tensor(rk_base[:], rkv, e_base[:].unsqueeze(1).broadcast_to([P, TPB, E]), ALU.add
                                    ).then_inc(r.slot, 1)
            nc.vector.tensor_copy(cum[:, 0, :], cum[:, TPB, :]).then_inc(r.slot, 1)
            eng.wait_ge(r.slot, 6 * b + 4)
            nc.vector.tensor_tensor(pick[:], ohb, rk_base[:].unsqueeze(2).broadcast_to([P, TPB, 2, E]), ALU.mult
                                    ).then_inc(r.slot, 1)
            eng.wait_ge(r.slot, 6 * b + 5)
            if live_b(b, 1):
                if r is r0:
                    eng.wait_ge(r.sent, SENT * b)
                else:
                    eng.wait_ge(r.free, b + 1)
            with nc.allow_low_precision(reason="row numbers below 2**24, exact in float32"):
                nc.vector.tensor_reduce(slot[:], pick[:], AXX, ALU.add).then_inc(r.slot, 1)

        def pool_send(eng, r, b, xn):
            eng.wait_ge(r.slot, 6 * b + 6)
            apart(eng)
            for i in range(TPB):
                for k in range(2):
                    nc.gpsimd.indirect_dma_start(
                        out=xs_dram[:, :],
                        out_offset=bass.IndirectOffsetOnAxis(
                            ap=slot[:, i, k:k + 1], axis=0),
                        in_=xn[:, i, :], in_offset=None).then_inc(r.sent, 16)

        SENT = 16 * 2 * TPB

        def pe_total(eng, r):
            eng.wait_ge(r.cum, TPB * B)
            eng.wait_ge(r.slot, 6 * B)
            nc.tensor.matmul(ps[:, 2, 0:E], ones[:], cum[:, TPB, :], start=True, stop=True).then_inc(r.total, 1)

        def dve_tables(eng, r):
            n = [0]

            def step(ins):
                ins.then_inc(r.t, 1)
                n[0] += 1
                eng.wait_ge(r.t, n[0])

            eng.wait_ge(r.total, 1)
            step(nc.vector.tensor_copy(cnt[:], ps[:, 2, 0:E]))
            step(nc.vector.tensor_tensor(padf[:], cnt[:], e_base[:], ALU.add))
            nc.vector.tensor_scalar(pad[:], padf[:], p_f[:, 0:1], None, ALU.add).then_inc(r.pad_ready, 1)
            nc.vector.memset(zrows, 0.0).then_inc(r.zero, 1)
            step(nc.vector.tensor_scalar(cnt_i[:], cnt[:], float(P - 1), None, ALU.add))
            step(nc.vector.tensor_scalar(cnt_i[:], cnt_i[:], 7, None, ALU.arith_shift_right))
            step(nc.vector.tensor_copy(nt[:], cnt_i[:]))
            step(nc.vector.tensor_tensor_scan(ends[:], nt[:], zero8[:], 0.0, ALU.add, ALU.add))
            step(nc.vector.tensor_tensor(start128[:], ends[:], nt[:], ALU.subtract))
            step(nc.vector.tensor_scalar(start128[:], start128[:], float(P), None, ALU.mult))
            step(nc.vector.tensor_tensor(abase[:], e_base[:], start128[:], ALU.subtract))
            step(nc.vector.memset(dbase[:], 0.0))
            step(nc.vector.tensor_tensor(dbase[:, 0:E - 1], abase[:, 1:E], abase[:, 0:E - 1], ALU.subtract))
            step(nc.vector.tensor_tensor(le[:], ends[:].unsqueeze(1).broadcast_to([P, TILES, E]),
                                         j_f[:].unsqueeze(2).broadcast_to([P, TILES, E]), ALU.is_le))
            step(nc.vector.tensor_reduce(ef[:], le[:], AXX, ALU.add))
            step(nc.vector.tensor_scalar(exp_tab[:], ef[:], float(E - 1), None, ALU.min))
            step(nc.vector.tensor_tensor(lep, le[:], dbase[:].unsqueeze(1).broadcast_to([P, TILES, E]), ALU.mult))
            step(nc.vector.tensor_reduce(tmpj[:], lep, AXX, ALU.add))
            step(nc.vector.scalar_tensor_tensor(rowf[:], j_f[:], float(P), tmpj[:], ALU.mult, ALU.add))
            step(nc.vector.tensor_scalar(tmpj[:], rowf[:], -1.0, float((E - 1) * REGION), ALU.mult, ALU.add))
            step(nc.vector.tensor_tensor(tmpj[:], tmpj[:], le[:, :, E - 1], ALU.mult))
            step(nc.vector.tensor_tensor(row_tab[:], rowf[:], tmpj[:], ALU.add))
            step(nc.vector.tensor_tensor(rk_y, rk[:], start128[:].unsqueeze(1).broadcast_to([P, T, E]), ALU.add))
            step(nc.vector.tensor_tensor(pick_y, oh[:], rk_y.unsqueeze(2).broadcast_to([P, T, 2, E]), ALU.mult))
            with nc.allow_low_precision(reason="row numbers below 2**24, exact in float32"):
                nc.vector.tensor_reduce(yslot[:], pick_y, AXX, ALU.add).then_inc(r.tabs, 1)
            nc.vector.memset(cum[:, 0, :], 0.0).then_inc(r.tabs, 1)
            eng.wait_ge(r.tabs, 2)

        def pool_pads(eng, r):
            eng.wait_ge(r.pad_ready, 1)
            eng.wait_ge(r.zero, 1)
            eng.wait_ge(r.sent, SENT * B)
            for e in range(E):
                nc.gpsimd.indirect_dma_start(
                    out=xs_dram[:, :], out_offset=bass.IndirectOffsetOnAxis(ap=pad[:, e:e + 1], axis=0),
                    in_=zrows, in_offset=None).then_inc(r.pad, 16)

        def expert_engines(q, r):
            STEPS = TILES + 6

            def steps(eng, body):
                for i in range(8):
                    body(i, i % 4)
                with eng.Fori(2, TILES // 4) as it:
                    for u in range(4):
                        body(it * 4 + u, u)
                for i in range(TILES, STEPS):
                    body(i, i % 4)

            def live(i, k):
                return not isinstance(i, int) or 0 <= i - k < TILES

            def ge(eng, s, v):
                if not isinstance(v, int) or v > 0:
                    eng.wait_ge(s, v)

            def turns(i, u, back):
                if isinstance(i, int):
                    return 16 * ((i - back) // 4 + 1)
                return (i - u) * 4 + 16 * ((u - back) // 4 + 1)

            def sp(eng):
                eng.wait_ge(r.tabs, 1)
                eng.wait_ge(r.pad, 16 * E)

                def body(i, u):
                    if live(i, 0):
                        ge(eng, q.tp, i - 3)
                        apart(eng)
                        row = eng.value_load(row_tab[0:1, ds(i, 1)], min_val=0, max_val=E * REGION - P)
                        eng.dma_start(xs[:, u, :], xs_dram[ds(row, P), :]).then_inc(q.ld[u], 16)
                    if live(i, 6):
                        ge(eng, q.ysb, i - 5)
                        w = (u - 6) % 4
                        apart(eng)
                        eng.dma_start(y_dram[ds((i - 6) * P, P), :], ysb[:, w, :]).then_inc(q.st[w], 16)
                steps(eng, body)
                for w in range(4):
                    eng.wait_ge(q.st[w], 16 * (TILES // 4))

            def pe(eng):
                eng.wait_ge(r.tabs, 1)
                eng.wait_ge(s_w, 32 if q is x0 else 48)

                def weights_of(tile):
                    return eng.value_load(exp_tab[0:1, ds(tile, 1)], min_val=0, max_val=E - 1)

                def body(i, u):
                    if live(i, 0):
                        ge(eng, q.xT, i - 1)
                        eng.wait_ge(q.ld[u], turns(i, u, 0))
                        for c in range(DC):
                            mm = nc.tensor.transpose(ps[:, u % 2, c * P:(c + 1) * P],
                                                     xs[:, u, c * P:(c + 1) * P], ident[:])
                        mm.then_inc(q.tp, 1)
                    if live(i, 1):
                        e = weights_of(i - 1)
                        w = (u + 1) % 2
                        ge(eng, q.xT, i)
                        ge(eng, q.relu, i - 2)
                        for c in range(DC):
                            mm = nc.tensor.matmul(ps[:, 2 + w, :], xsT[:, w, c * P:(c + 1) * P],
                                                  w1s[:, ds(e, 1), c:c + 1, :].rearrange("p a b f -> p (a b f)"),
                                                  start=(c == 0), stop=(c == DC - 1))
                        mm.then_inc(q.h, 1)
                    if live(i, 2):
                        w = u % 2
                        ge(eng, q.relu, i - 1)
                        ge(eng, q.hT, i - 3)
                        for c in range(FC):
                            mm = nc.tensor.transpose(ps[:, 4 + w, c * P:(c + 1) * P],
                                                     hid[:, w, c * P:(c + 1) * P], ident[:])
                        mm.then_inc(q.hTp, 1)
                    if live(i, 3):
                        e = weights_of(i - 3)
                        w = (u + 1) % 2
                        ge(eng, q.hT, i - 2)
                        ge(eng, q.ysb, i - 4)
                        for c in range(FC):
                            mm = nc.tensor.matmul(ps[:, 6 + w, 0:D], hidT[:, w, c * P:(c + 1) * P],
                                                  w2s[:, ds(e, 1), c:c + 1, :].rearrange("p a b f -> p (a b f)"),
                                                  start=(c == 0), stop=(c == FC - 1))
                        mm.then_inc(q.y, 1)
                steps(eng, body)

            def act(eng):
                def body(i, u):
                    if live(i, 0):
                        eng.wait_ge(q.tp, i + 1)
                        ge(eng, q.h, i - 1)
                        nc.scalar.copy(xsT[:, u % 2, :], ps[:, u % 2, 0:D]).then_inc(q.xT, 1)
                    if live(i, 1):
                        w = (u + 1) % 2
                        ge(eng, q.h, i)
                        ge(eng, q.hTp, i - 2)
                        nc.scalar.activation(hid[:, w, :], ps[:, 2 + w, :], ACT.Relu).then_inc(q.relu, 1)
                steps(eng, body)

            def dve(eng):
                def body(i, u):
                    if live(i, 2):
                        w = u % 2
                        ge(eng, q.hTp, i - 1)
                        ge(eng, q.y, i - 3)
                        nc.vector.tensor_copy(hidT[:, w, :], ps[:, 4 + w, :]).then_inc(q.hT, 1)
                    if live(i, 3):
                        w, v = (u + 1) % 2, (u + 1) % 4
                        ge(eng, q.y, i - 2)
                        if not isinstance(i, int) or i >= 7:
                            eng.wait_ge(q.st[v], turns(i, u, 7))
                        nc.vector.tensor_copy(ysb[:, v, :], ps[:, 6 + w, 0:D]).then_inc(q.ysb, 1)
                steps(eng, body)

            return sp, pe, act, dve

        e0, e1 = expert_engines(x0, r0), expert_engines(x1, r1)

        def pool_gather(eng, l, t, u, half):
            if not isinstance(t, int) or t >= 2:
                eng.wait_ge(s_comb[l], t - 1)
            nc.gpsimd.tensor_copy(yidx[:, u:u + 1, :], yslot[:, ds(t, 1), :]).then_inc(s_idx[l], 1)
            eng.wait_ge(s_idx[l], t + 1)
            apart(eng)
            for k in range(2):
                nc.gpsimd.indirect_dma_start(
                    out=yg[:, u, k, :], out_offset=None, in_=y_dram[:, :],
                    in_offset=bass.IndirectOffsetOnAxis(
                        ap=yidx[:, u, k:k + 1], axis=0)
                ).then_inc(s_gath[l][u], 16)

        def dve_combine(eng, l, t, u, half):
            eng.wait_ge(s_gath[l][u], half * 32 + 32)
            xt = x[:, ds(t, 1), :].rearrange("p o d -> p (o d)")
            w = wts[:, ds(t, 1), :].rearrange("p o k -> p (o k)")
            nc.vector.scalar_tensor_tensor(xt, yg[:, u, 0, :], w[:, 0:1], xt, ALU.mult, ALU.add
                                           ).then_inc(s_comb_half[l], 1)
            eng.wait_ge(s_comb_half[l], t + 1)
            nc.vector.scalar_tensor_tensor(xt, yg[:, u, 1, :], w[:, 1:2], xt, ALU.mult, ALU.add
                                           ).then_inc(s_comb[l], 1)

        def pool_early(eng, b):
            if live_b(b, 1):
                eng.wait_ge(s_part, 128 * b)
            for i in range(TPB):
                pool_gather(eng, 0, b * TPB + i, i % 2, b * 2 + i // 2)
            pool_norm(eng, npr, b)
            eng.wait_ge(npr.xn, TPB * b + TPB)
            xb = x[:, ds(b * TPB, TPB), :]
            nc.gpsimd.tensor_tensor(xb, xb, bo[:].unsqueeze(1).broadcast_to([P, TPB, D]), ALU.add
                                    ).then_inc(s_bias, 1)

        def dve_early_stats(eng, b):
            eng.wait_ge(s_comb[0], b * TPB + TPB)
            dve_stats(eng, npr, b)

        def dve_early_rows(eng, b):
            dve_rows(eng, npr, b, xn_p, (lambda: eng.wait_ge(s_part, 128 * b)) if live_b(b, 1) else None)

        def dve_prep(eng, b, bb):
            dve_norm_copy(eng, npr, b)
            for c in range(2):
                for n in range(2):
                    eng.wait_ge(s_hi, 4 * b + 2 * c + n + 1)
                    nc.vector.scalar_tensor_tensor(
                        part[:, 2 * n + 1, :], ps[:, n, :], bcol[:, c, n:n + 1],
                        part[:, 2 * n, :].bitcast(F32), ALU.add, ALU.subtract).then_inc(s_lo, 1)
                    if c == 0 and n == 0 and bb is not None:
                        dve_normalise(eng, 4 * bb + 3, ubuf(bb, 1), 1)
                eng.wait_ge(s_v, 2 * b + c + 1)
                nc.vector.tensor_tensor(
                    vs[:, vbuf(b), 2 * c:2 * c + 2, :, 0:DH],
                    ps[:, 2 + c, :].rearrange("p (i h d) -> p i h d", i=2, h=H),
                    bv[:].unsqueeze(1).broadcast_to([P, 2, H, DH]), ALU.add).then_inc(s_vs, 1)
                if c == 0 and bb is not None:
                    dve_attnT(eng, bb)

        def act_prep(eng, b, bb):
            act_norm(eng, npr, b)
            for c in range(2):
                if c == 1 and bb is not None:
                    act_attnT(eng, bb)
                for n in range(2):
                    eng.wait_ge(s_qk, 4 * b + 2 * c + n + 1)
                    if n == 0 and (c or live_b(b, 1)):
                        eng.wait_ge(s_part, 64 * (2 * b + c))
                    nc.scalar.activation(part[:, 2 * n, :], ps[:, n, :], ACT.Identity, bias=bcol[:, c, n:n + 1]
                                         ).then_inc(s_hi, 1)

        def pe_prep(eng, b, bb):
            if live_b(b, 1):
                eng.wait_ge(s_red, 16 * (2 * b - 1))
            pe_norm(eng, npr, b, xn_p)
            eng.wait_ge(npr.ev0, b + 1)
            eng.wait_ge(npr.ev1, b + 1)
            for c in range(2):
                if c and bb is not None:
                    pe_attnT(eng, bb)
                for n in range(2):
                    if c:
                        eng.wait_ge(s_lo, 4 * b + n + 1)
                    for k in range(DC):
                        mm = nc.tensor.matmul(ps[:, n, :], wqkv[:, k, n, P * c:P * c + P], xT[:, k, :],
                                              start=(k == 0), stop=(k == DC - 1))
                    mm.then_inc(s_qk, 1)
                if c == 0 and bb is not None:
                    eng.wait_ge(s_mev, 2 * b - 1)
                    pe_heads(eng, 4 * bb + 3, 1)
                for i in range(2 * c, 2 * c + 2):
                    o = ps[:, 2 + i // 2, (i % 2) * D:(i % 2) * D + D]
                    for k in range(DC):
                        mm = nc.tensor.matmul(o, xT[:, k, i * P:(i + 1) * P], wqkv[:, k, 2, :],
                                              start=(k == 0), stop=(k == DC - 1))
                mm.then_inc(s_v, 1)

        def sp_parts(eng, b, c):
            if live_b(b, 1):
                eng.wait_ge(s_ld[c], 192 * b)
                apart(eng)
            for n in range(2):
                eng.wait_ge(s_hi, 4 * b + 2 * c + n + 1)
                eng.dma_start(qk_dram[c, 2 * n], part[:, 2 * n, :].bitcast(F32)).then_inc(s_part, 16)
                eng.wait_ge(s_lo, 4 * b + 2 * c + n + 1)
                eng.dma_start(qk_dram[c, 2 * n + 1], part[:, 2 * n + 1, :].bitcast(F32)).then_inc(s_part, 16)
            eng.wait_ge(s_part, 64 * (2 * b + c + 1))

        def sp_stack(eng, b, c, u3):
            if live_b(b, 2):
                eng.wait_ge(s_sc, 32 * (2 * b + c - 3))
            rows = [(qst, 0, 0), (qst, 1, 0), (qst, 2, 1), (kst, 0, 2), (kst, 1, 3), (kst, 2, 2)]
            for dst, row, src in rows:
                for par in range(2):
                    p0 = 64 * par + DH * row
                    eng.dma_start(dst[p0:p0 + DH, u3, :, :].bitcast(F32),
                                  qk_dram[c, src].rearrange("(g r d) n -> r d g n", r=2, d=DH)[par]
                                  ).then_inc(s_ld[c], 16)

        def live_b(b, n):
            return b >= n if isinstance(b, int) else True

        def pe_max_tile(b, c, u3, s):
            pair, par, qt = s // 8, s % 2, (s % 8) // 2
            p0 = 64 * par
            return nc.tensor.matmul(ps[:, s % 4, :], qst[p0:p0 + 3 * DH, u3, pair, qt * P:(qt + 1) * P],
                                    kst[p0:p0 + 3 * DH, u3, pair, :], start=True, stop=True)

        def pe_pv(eng, b, c, m):
            g, kt = m // 4, m % 4
            U8 = 8 * (2 * b + c)
            eng.wait_ge(s_exp, 4 * (U8 + m) + 4)
            if kt == 0 and (g or c or live_b(b, 1)):
                eng.wait_ge(s_oev, 2 * (2 * b + c) + g)
            for hh in range(4):
                h = c * HU + 4 * g + hh
                mm = nc.tensor.matmul(ps[32 * hh:32 * hh + VW, O_BANK, :], vs[:, vbuf(b), kt, h, :],
                                      probs[:, (4 * m + hh) % 16, :], start=(kt == 0), stop=(kt == 3))
            mm.then_inc(s_pv, 1)

        def pe_heads(eng, n, slot_):
            eng.wait_ge(s_oev, n + 1)
            for qt in range(TPB):
                mm = nc.tensor.transpose(ps[:, T_BANK, qt * P:(qt + 1) * P], osb[:, slot_, qt * P:(qt + 1) * P],
                                         ident[:])
            mm.then_inc(s_otr, 1)

        LEAD = 2

        def pe_unit(eng, b, c, nxt, routed=None):
            U = None if b is None else 2 * b + c
            if nxt is not None:
                nb, ncx, nu4 = nxt
                NU = 2 * nb + ncx
                eng.wait_ge(s_ld[ncx], 192 * nb + 192)

            def maxima(t):
                if nxt is None or t >= 32:
                    return
                if t % 2 == 0 and (t >= 4 or ncx or live_b(nb, 1)):
                    eng.wait_ge(s_red, 16 * NU + t // 2 - 1)
                mm = pe_max_tile(nb, ncx, nu4, t)
                if t % 2 == 1:
                    mm.then_inc(s_mm, 1)

            for t in range(LEAD):
                maxima(t)
            if b is not None:
                eng.wait_ge(s_mrow[c], 32 * b + 32)
                if c == 0:
                    eng.wait_ge(s_vs, 2 * b + 2)
                    if not (isinstance(b, int) and b == 0):
                        eng.wait_ge(s_x2, 2 * b)
            for s in range(32):
                maxima(s + LEAD)
                if b is None:
                    continue
                if s >= 2 or c or live_b(b, 1):
                    eng.wait_ge(s_exp, 32 * U + s - 1)
                g, kt, hh = s // 16, (s % 16) // 4, s % 4
                pair, par = 2 * g + hh // 2, hh % 2
                p0 = 64 * par
                nc.tensor.matmul(ps[:, 4 + s % 2, :], kst[p0:p0 + 3 * DH + 1, ubuf(b, c), pair, kt * P:(kt + 1) * P],
                                 qst[p0:p0 + 3 * DH + 1, ubuf(b, c), pair, :], start=True, stop=True
                                 ).then_inc(s_sc, 1)
                if s % 8 == 3 and s >= 11:
                    pe_pv(eng, b, c, s // 4 - 2)
                    pe_pv(eng, b, c, s // 4 - 1)
                if s == 14 and c:
                    eng.wait_ge(s_mev, U + 1)
                    pe_heads(eng, 2 * U - 1, 1)
                if routed is not None:
                    if s == 9:
                        eng.wait_ge(s_at, 2 * U)
                        pe_norm(eng, r1.norm, routed, xn_r, chunks=(0,), banks=(7, 7))
                    if s == 13:
                        eng.wait_ge(r1.norm.ev0, routed + 1)
                        pe_norm(eng, r1.norm, routed, xn_r, chunks=(1,), banks=(7, 7))
                    if s == 19:
                        pe_logits(eng, r1, routed)
                    if s == 25:
                        pe_ranks(eng, r1, routed)
                if s == 28:
                    if routed is not None:
                        eng.wait_ge(r1.slot, 6 * routed + 4)
                    if not (c or live_b(b, 1)):
                        eng.wait_ge(s_mev, U + 1)
                    else:
                        eng.wait_ge(s_at, 2 * U)
                    pe_heads(eng, 2 * U, 0)
            if b is not None:
                pe_pv(eng, b, c, 6)
            if nxt is not None:
                if b is not None:
                    eng.wait_ge(s_at, 2 * U + 1)
                eng.wait_ge(s_red, 16 * NU + 16)
                nc.tensor.transpose(ps[0:32, T_BANK, 0:P], mx[:], ident[:]).then_inc(s_mtr, 1)
            if b is not None:
                pe_pv(eng, b, c, 7)

        def act_unit(eng, b, c, nxt, routed=None):
            U = None if b is None else 2 * b + c

            def heads_copy(g):
                eng.wait_ge(s_pv, 8 * U + 4 * g + 4)
                if not (isinstance(U, int) and 2 * U + g < 2):
                    eng.wait_ge(s_otr, 2 * U + g - 1)
                nc.scalar.copy(osb[:, g, :], ps[:, O_BANK, :]).then_inc(s_oev, 1)

            if b is not None:
                for s in range(32):
                    eng.wait_ge(s_sc, 32 * U + s + 1)
                    if s >= 16 or c or live_b(b, 1):
                        eng.wait_ge(s_pv, 8 * U + s // 4 - 3)
                    nc.scalar.activation(probs[:, s % 16, :], ps[:, 4 + s % 2, :], ACT.Exp, scale=LOGIT_SCALE
                                         ).then_inc(s_exp, 1)
                    if s == 24:
                        heads_copy(0)
                    if routed is not None and s == 10:
                        act_norm(eng, r1.norm, routed, bank=7)
                    if routed is not None and s == 22:
                        act_route(eng, r1, routed)
            if nxt is not None:
                nb, ncx, nu4 = nxt
                NU = 2 * nb + ncx
                eng.wait_ge(s_mtr, NU + 1)
                if live_b(nb, 1) or ncx:
                    if ncx:
                        eng.wait_ge(s_mrow[0], 32 * nb + 32)
                    else:
                        eng.wait_ge(s_mrow[1], 32 * nb)
                nc.scalar.activation(mT[:], ps[0:32, T_BANK, 0:P], ACT.Copy, scale=-1.0).then_inc(s_mev, 1)
                eng.wait_ge(s_mev, NU + 1)
                for par in range(2):
                    r = 64 * par + 3 * DH
                    eng.dma_start(qst[r:r + 1, nu4, :, :].bitcast(F32), mT[16 * par:16 * par + 16, :].bitcast(F32)
                                  ).then_inc(s_mrow[ncx], 16)
            if b is not None:
                heads_copy(1)

        def dve_normalise(eng, n, u4, g):
            eng.wait_ge(s_otr, n + 1)
            o = ps[:, T_BANK, :].rearrange("p (q h w) -> p q h w", q=TPB, h=4)
            if not (isinstance(n, int) and n == 0):
                eng.wait_ge(s_at, n)
            nc.vector.reciprocal(rs[:].unsqueeze(3), o[:, :, :, DH:DH + 1]).then_inc(s_rec, 1)
            eng.wait_ge(s_rec, n + 1)
            dst = attn[:, u4, :, 64 * g:64 * g + 64].rearrange("p q (h d) -> p q h d", h=4)
            nc.vector.tensor_tensor(dst, o[:, :, :, 0:DH], rs[:].unsqueeze(3).broadcast_to([P, TPB, 4, DH]),
                                    ALU.mult).then_inc(s_at, 1)

        def dve_unit(eng, b, c, nxt, routed=None, early=None):
            U = None if b is None else 2 * b + c
            for j in range(16):
                if nxt is not None:
                    nb, ncx, nu4 = nxt
                    NU = 2 * nb + ncx
                    if j == 0 and (ncx or live_b(nb, 1)):
                        eng.wait_ge(s_mtr, NU)
                    eng.wait_ge(s_mm, 16 * NU + j + 1)
                    dst = mx[:].rearrange("p (r c) -> p r c", r=2)[:, :, j:j + 1]
                    bk = (2 * j) % 4
                    nc.vector.tensor_reduce(dst, ps[:, bk:bk + 2, :].unsqueeze(2), AXX, ALU.max
                                            ).then_inc(s_red, 1)
                if early is not None:
                    if j in (7, 8, 11, 12):
                        i = (7, 8, 11, 12).index(j)
                        dve_combine(eng, 0, early * TPB + i, i % 2, early * 2 + i // 2)
                    if j == 13:
                        dve_early_stats(eng, early)
                    if j == 15:
                        dve_early_rows(eng, early)
                if routed is not None:
                    if j == 0:
                        dve_stats(eng, r1.norm, routed)
                    if j == 2:
                        dve_rows(eng, r1.norm, routed, xn_r,
                                 (lambda: eng.wait_ge(r1.free, routed + 1)) if live_b(routed, 1) else None)
                    if j == 7:
                        dve_norm_copy(eng, r1.norm, routed, bank=7)
                    if j >= 10 and j < 15:
                        (dve_top2, dve_onehots, dve_counts, dve_weights, dve_slots)[j - 10](eng, r1, routed)
                if b is None:
                    continue
                if j == 8 and c:
                    dve_normalise(eng, 2 * U - 1, ubuf(b, 0), 1)
                if j == 15:
                    dve_normalise(eng, 2 * U, ubuf(b, c), 0)

        def pe_attnT(eng, b):
            eng.wait_ge(s_at, 4 * b + 4)
            for c in range(DC):
                for qt in range(TPB):
                    mm = nc.tensor.transpose(ps[:, 4 + c, qt * P:(qt + 1) * P], attn[:, ubuf(b, c), qt, :], ident[:])
                mm.then_inc(s_ptr, 1)

        def act_attnT(eng, b):
            eng.wait_ge(s_ptr, 2 * b + 1)
            nc.scalar.copy(osb[:, 0, :], ps[:, 4, :]).then_inc(s_pev0, 1)

        def dve_attnT(eng, b):
            eng.wait_ge(s_ptr, 2 * b + 2)
            nc.vector.tensor_copy(osb[:, 1, :], ps[:, 5, :]).then_inc(s_pev1, 1)

        def pe_project(eng, b):
            eng.wait_ge(s_pev0, b + 1)
            eng.wait_ge(s_pev1, b + 1)
            for i in range(TPB):
                o = ps[:, 4 + i // 2, (i % 2) * D:(i % 2) * D + D]
                for k in range(DC):
                    mm = nc.tensor.matmul(o, osb[:, k, i * P:(i + 1) * P], wout[:, k, :],
                                          start=(k == 0), stop=(k == DC - 1))
                if i % 2:
                    mm.then_inc(s_prj, 1)

        def dve_project(eng, b):
            eng.wait_ge(s_bias, b + 1)
            for j in range(2):
                eng.wait_ge(s_prj, 2 * b + j + 1)
                xb = x[:, ds(b * TPB + 2 * j, 2), :]
                nc.vector.tensor_tensor(xb, ps[:, 4 + j, :].rearrange("p (i d) -> p i d", i=2), xb, ALU.add
                                        ).then_inc(s_x2, 1)
            eng.wait_ge(s_x2, 2 * b + 2)

        def pool_post(eng, b):
            pool_norm(eng, r1.norm, b)
            pool_send(eng, r1, b, xn_r)
            eng.wait_ge(r1.sent, SENT * b + SENT)
            eng.sem_inc(r1.free, 1)

        parity = {}

        def vbuf(b):
            return b % 2 if isinstance(b, int) else parity[id(b)]

        def ubuf(b, c):
            return 2 * vbuf(b) + c

        kept = []

        def attention(eng, prep, unit, project):
            def turn(b, before, after):
                unit(before, 1, (b, 0, ubuf(b, 0)), None, after)
                if after is not None:
                    prep(after, before)
                project(before, after)
                unit(b, 0, (b, 1, ubuf(b, 1)), before, None)

            prep(0, None)
            unit(None, 0, (0, 0, ubuf(0, 0)), None, 1)
            prep(1, None)
            unit(0, 0, (0, 1, ubuf(0, 1)), None, None)
            with eng.Fori(0, (B - 2) // 2) as it:
                for j in range(2):
                    numbers = [it * 2 + (1 + j + d) if 1 + j + d else it * 2 for d in (0, -1, 1)]
                    for v, d in zip(numbers, (0, -1, 1)):
                        parity[id(v)] = (1 + j + d) % 2
                    kept.append(numbers)
                    turn(*numbers)
            turn(B - 1, B - 2, None)
            unit(B - 1, 1, None, None, None)
            project(B - 1, None)

        def route0(eng, turn):
            turn(0, 0, True)
            with eng.Fori(0, (B - 2) // 2) as it:
                turn(it * 2 + 1, 1, True)
                turn(it * 2 + 2, 0, True)
            turn(B - 1, (B - 1) % 2, False)

        xn0 = (xn_r, attn[:].rearrange("p a q n -> p (a q n)")[:, 0:TPB * D].rearrange("p (i d) -> p i d", d=D))

        def dve_route0(eng, g, par, more):
            if more:
                eng.wait_ge(s_x, g * 16 + 32)
                dve_stats(eng, r0.norm, g + 1)
            for stage in (dve_top2, dve_onehots, dve_counts, dve_weights):
                stage(eng, r0, g)
            if more:
                dve_rows(eng, r0.norm, g + 1, xn0[1 - par],
                         (lambda: eng.wait_ge(r0.sent, SENT * g)) if live_b(g, 1) else None)
            dve_slots(eng, r0, g)
            if more:
                dve_norm_copy(eng, r0.norm, g + 1)

        def pool_route0(eng, g, par, more):
            if more:
                pool_norm(eng, r0.norm, g + 1)
            pool_send(eng, r0, g, xn0[par])

        def act_route0(eng, g, par, more):
            act_route(eng, r0, g)
            if more:
                act_norm(eng, r0.norm, g + 1)

        def pe_route0(eng, g, par, more):
            if live_b(g, 1):
                eng.wait_ge(r0.slot, 6 * g)
            pe_ranks(eng, r0, g)
            if more:
                pe_norm(eng, r0.norm, g + 1, xn0[1 - par])
                pe_logits(eng, r0, g + 1)

        @block.sync
        def _(eng):
            with eng.Fori(0, B) as g:
                eng.dma_start(x[:, ds(g * TPB, TPB), :], x_tok[:, ds(g * TPB, TPB), :]).then_inc(s_x, 16)
                eng.wait_ge(s_x, g * 16 + 16)
                apart(eng)
            e0[0](eng)

            def prep(b, _):
                for c in range(2):
                    sp_parts(eng, b, c)
                    sp_stack(eng, b, c, ubuf(b, c))
            attention(eng, prep, lambda *a: None, lambda *a: None)
            eng.wait_ge(s_pv, 8 * 2 * B)
            eng.dma_start(w2s[:], w2.rearrange("e (c p) f -> p e c f", p=P)).then_inc(s_w, 16)
            e1[0](eng)
            with eng.Fori(0, T) as t:
                eng.wait_ge(s_comb[1], t + 1)
                apart(eng)
                eng.dma_start(out_tok[:, ds(t, 1), :], x[:, ds(t, 1), :]).then_inc(s_out, 16)
            eng.wait_ge(s_out, 16 * T)

        @block.gpsimd
        def _(eng):
            nc.gpsimd.iota(e_i[:], pattern=[[1, E]], base=0, channel_multiplier=0).then_inc(s_iota, 1)
            nc.gpsimd.iota(p_i[:], pattern=[[0, 1]], base=0, channel_multiplier=1).then_inc(s_iota, 1)
            nc.gpsimd.iota(j_i[:], pattern=[[1, TILES]], base=0, channel_multiplier=0).then_inc(s_iota, 1)
            nc.gpsimd.memset(ident[:], 0.0).then_inc(s_iota, 1)
            nc.gpsimd.memset(ones[:], 1.0).then_inc(s_iota, 1)
            nc.gpsimd.memset(mhalf[:], -0.5).then_inc(s_const, 1)
            eng.sem_inc(r1.free, 1)
            eng.wait_ge(s_iota, 5)
            nc.gpsimd.affine_select(out=ident[:], in_=ident[:], compare_op=ALU.not_equal, fill=1.0, base=0,
                                    pattern=[[-1, P]], channel_multiplier=1).then_inc(s_const, 1)
            nc.gpsimd.affine_select(out=upper[:], in_=ones[:], compare_op=ALU.is_gt, fill=0.0, base=0,
                                    pattern=[[1, P]], channel_multiplier=-1).then_inc(s_const, 1)
            eng.wait_ge(s_const, 3)
            pool_norm(eng, r0.norm, 0)
            route0(eng, lambda g, par, more: pool_route0(eng, g, par, more))
            pool_pads(eng, r0)
            eng.wait_ge(s_small, SMALL)
            for c in range(DC):
                for n in range(3):
                    nc.gpsimd.tensor_copy(
                        wqkv[:, c, n, :].rearrange("p (h d) -> p h d", h=H),
                        wraw[:, c, :].rearrange("p (h n d) -> p n h d", n=3, d=DH)[:, n]).then_inc(s_sorted, 1)
            eng.wait_ge(s_sorted, 3 * DC)
            nc.gpsimd.memset(vs[:], 1.0).then_inc(s_sorted, 1)
            for w in range(4):
                eng.wait_ge(x0.st[w], 16 * (TILES // 4))

            pool_early(eng, 0)

            def unit(b, c, nxt, routed, early):
                if early is not None:
                    pool_early(eng, early)
                if routed is not None:
                    pool_post(eng, routed)
            attention(eng, lambda *a: None, unit, lambda *a: None)
            pool_post(eng, B - 1)
            pool_pads(eng, r1)
            for w in range(4):
                eng.wait_ge(x1.st[w], 16 * (TILES // 4))
            for t in range(2):
                pool_gather(eng, 1, t, t, 0)
            with eng.Fori(1, T // 2) as it:
                for u in range(2):
                    pool_gather(eng, 1, it * 2 + u, u, it)

        @block.scalar
        def _(eng):
            with nc.allow_non_contiguous_dma(reason="bias columns"):
                eng.dma_start(wg[:], w_gate.rearrange("(c p) e -> p c e", p=P)).then_inc(s_wg, 16)
                eng.dma_start(wraw,
                              w_qkv.rearrange("(c p) n -> p c n", p=P)).then_inc(s_small, 16)
                eng.dma_start(wout[:], w_out.rearrange("(c p) n -> p c n", p=P)).then_inc(s_small, 16)
                bq = b_qkv.rearrange("(c h n d) -> n c h d", c=2, n=3, d=DH)
                for n in range(2):
                    for c in range(2):
                        for h in range(HU):
                            eng.dma_start(bcol[DH * h:DH * h + DH, c, n:n + 1],
                                          bq[n, c, h].unsqueeze(1)).then_inc(s_small, 16)
                eng.dma_start(bv[:], b_qkv.rearrange("(o h n d) -> n o h d", o=1, n=3, d=DH)[2]
                              .broadcast_to([P, H, DH])).then_inc(s_small, 16)
                eng.dma_start(bo[:], b_out.rearrange("(o d) -> o d", o=1).broadcast_to([P, D])
                              ).then_inc(s_small, 16)
            eng.dma_start(w1s[:], w1.rearrange("e (c p) f -> p e c f", p=P)).then_inc(s_w, 16)
            eng.dma_start(w2s[:], w2.rearrange("e (c p) f -> p e c f", p=P)).then_inc(s_w, 16)

            act_norm(eng, r0.norm, 0)
            route0(eng, lambda g, par, more: act_route0(eng, g, par, more))
            e0[2](eng)

            attention(eng, lambda b, bb: act_prep(eng, b, bb),
                      lambda b, c, nxt, routed, early: act_unit(eng, b, c, nxt, routed),
                      lambda b, nb: act_attnT(eng, b) if nb is None else None)
            act_norm(eng, r1.norm, B - 1, bank=7)
            act_route(eng, r1, B - 1)
            e1[2](eng)

        @block.tensor
        def _(eng):
            eng.wait_ge(s_const, 3)
            eng.wait_ge(s_dve0, NCONST)
            eng.wait_ge(s_wg, 16)
            pe_norm(eng, r0.norm, 0, xn_r)
            pe_logits(eng, r0, 0)
            route0(eng, lambda g, par, more: pe_route0(eng, g, par, more))
            eng.wait_ge(s_small, SMALL)
            pe_total(eng, r0)
            e0[1](eng)
            eng.wait_ge(s_sorted, 3 * DC + 1)
            eng.wait_ge(x0.ysb, TILES)
            for done in (x0.xT, x0.relu, x0.hT):
                eng.wait_ge(done, TILES)
            eng.wait_ge(s_dve0, NCONST + 1)

            def project(b, nb):
                if nb is None:
                    if b != B - 1:
                        eng.wait_ge(s_mev, 2 * b + 3)
                    else:
                        eng.wait_ge(s_at, 4 * b + 3)
                    pe_heads(eng, 4 * b + 3, 1)
                    pe_attnT(eng, b)
                pe_project(eng, b)
                if nb is not None:
                    qkv_read(nb)

            def qkv_read(b):
                eng.wait_ge(s_lo, 4 * b + 4)
                eng.wait_ge(s_hi, 4 * b + 4)
                eng.wait_ge(s_vs, 2 * b + 2)

            def prep(b, bb):
                pe_prep(eng, b, bb)
                if bb is None:
                    qkv_read(b)
            attention(eng, prep, lambda b, c, nxt, routed, early: pe_unit(eng, b, c, nxt, routed), project)
            pe_norm(eng, r1.norm, B - 1, xn_r, chunks=(0,), banks=(7, 7))
            eng.wait_ge(r1.norm.ev0, B)
            pe_norm(eng, r1.norm, B - 1, xn_r, chunks=(1,), banks=(7, 7))
            pe_logits(eng, r1, B - 1)
            pe_ranks(eng, r1, B - 1)
            pe_total(eng, r1)
            e1[1](eng)

        @block.vector
        def _(eng):
            eng.wait_ge(s_iota, 3)
            nc.vector.tensor_copy(e_f[:], e_i[:]).then_inc(s_dve0, 1)
            nc.vector.tensor_copy(p_f[:], p_i[:]).then_inc(s_dve0, 1)
            nc.vector.tensor_copy(j_f[:], j_i[:]).then_inc(s_dve0, 1)
            nc.vector.memset(zero8[:], 0.0).then_inc(s_dve0, 1)
            nc.vector.memset(cum[:, 0, :], 0.0).then_inc(s_dve0, 1)
            nc.vector.memset(kst[:].bitcast(F32), 1.0).then_inc(s_dve0, 1)
            nc.vector.memset(ps[:, O_BANK, :], 0.0).then_inc(s_dve0, 1)
            eng.wait_ge(s_dve0, 1)
            nc.vector.tensor_scalar(e_base[:], e_f[:], float(REGION), None, ALU.mult).then_inc(s_dve0, 1)
            eng.wait_ge(s_dve0, NCONST)

            eng.wait_ge(s_x, 16)
            dve_norm(eng, r0.norm, 0, xn_r)
            dve_norm_copy(eng, r0.norm, 0)
            route0(eng, lambda g, par, more: dve_route0(eng, g, par, more))
            dve_tables(eng, r0)
            e0[3](eng)
            eng.wait_ge(x0.ysb, TILES)
            nc.vector.memset(ps[:, O_BANK, :], 0.0).then_inc(s_dve0, 1)
            eng.wait_ge(s_small, SMALL)

            for i in range(TPB):
                dve_combine(eng, 0, i, i % 2, i // 2)
            dve_early_stats(eng, 0)
            dve_early_rows(eng, 0)

            def prep(b, bb):
                dve_prep(eng, b, bb)

            def project(b, nb):
                if nb is None:
                    dve_normalise(eng, 4 * b + 3, ubuf(b, 1), 1)
                    dve_attnT(eng, b)
                dve_project(eng, b)
            attention(eng, prep, lambda b, c, nxt, routed, early: dve_unit(eng, b, c, nxt, routed, early), project)
            dve_norm(eng, r1.norm, B - 1, xn_r, lambda: eng.wait_ge(r1.free, B))
            dve_norm_copy(eng, r1.norm, B - 1, bank=7)
            for stage in (dve_top2, dve_onehots, dve_counts, dve_weights, dve_slots):
                stage(eng, r1, B - 1)
            dve_tables(eng, r1)
            e1[3](eng)
            for t in range(2):
                dve_combine(eng, 1, t, t, 0)
            with eng.Fori(1, T // 2) as it:
                for u in range(2):
                    dve_combine(eng, 1, it * 2 + u, u, it)


_INS = ['L0_attn_X', 'L0_attn_W_qkv', 'L0_attn_b_qkv', 'L0_attn_W_out', 'L0_attn_b_out',
        'L0_ffn_Wg', 'L0_ffn_W1', 'L0_ffn_W2']


def kernel(**inputs):
    import concourse.bacc as bacc
    from concourse.bass_utils import run_bass_kernel_spmd

    nc = bacc.Bacc("TRN2", target_bir_lowering=False, num_devices=1, dynamic_dma_scratch_size=4096)
    arrays, args = {}, []
    for name in _INS:
        a = np.ascontiguousarray(inputs[name])
        arrays[f"in_{name}"] = a
        args.append(nc.dram_tensor(f"in_{name}", a.shape, mybir.dt.from_np(a.dtype), kind="ExternalInput").ap())
    shape = inputs['L0_attn_X'].shape
    args.append(nc.dram_tensor("out_0", shape, F32, kind="ExternalOutput").ap())
    macaron_kernel(nc, *args)
    r = run_bass_kernel_spmd(nc, [arrays], core_ids=[0])
    return r.results[0]["out_0"]
```

```python
from contextlib import ExitStack

import numpy as np
import concourse.bass as bass
from concourse import mybir

P = 128
F32 = mybir.dt.float32
F32R = mybir.dt.float32r
U32 = mybir.dt.uint32
I32 = mybir.dt.int32
ACT = mybir.ActivationFunctionType
ALU = mybir.AluOpType
AXX = mybir.AxisListType.X
ds = bass.ds


def macaron_kernel(nc, x_in, w_qkv, b_qkv, w_out, b_out, w_gate, w1, w2, out):
    B, S, D = x_in.shape
    E, _, F = w1.shape
    H = 16
    DH = D // H
    TPB = S // P
    T = B * TPB
    DC = D // P
    FC = F // P
    G4 = TPB * E
    REGION = T * P + P
    TILES = -(-(2 * T + E - 1) // 4) * 4
    HU = H // 2
    PAIRS = HU // 2
    VW = DH + 1
    LOGIT_SCALE = 1.0 / float(np.sqrt(DH))
    assert S == 512 and D == 256 and E == 8 and TPB == 4

    x_tok = x_in.rearrange("b (i p) d -> p (b i) d", p=P)
    out_tok = out.rearrange("b (i p) d -> p (b i) d", p=P)

    xs_dram = nc.dram_tensor("xs_lists", [E * REGION, D], F32, kind="Internal").ap()
    y_dram = nc.dram_tensor("y_tiles", [TILES * P, D], F32, kind="Internal").ap()
    qk_dram = nc.dram_tensor("qk_parts", [2, 4, P, S], F32, kind="Internal").ap()

    with ExitStack() as ctx:
        def sb(name, shape, dt=F32):
            return ctx.enter_context(nc.sbuf_tensor(name, shape, dt))

        def sem(name):
            return ctx.enter_context(nc.semaphore(name))

        x = sb("x", [P, T, D])
        w1s = sb("w1s", [P, E, DC, F])
        w2s = sb("w2s", [P, E, FC, D])
        kst = sb("kst", [P, 3, HU, S], F32R)
        qst = sb("qst", [P, 3, PAIRS, S], F32R)
        probs = w2s[:].rearrange("p e c d -> p (e c d)").rearrange("p (r s) -> p r s", s=S)
        vs = sb("vs", [P, 3, TPB, H, VW])
        osb = sb("osb", [P, 2, S])
        attn = sb("attn", [P, 2, TPB, P])
        xT = sb("xT", [P, DC, S])
        wqkv = sb("wqkv", [P, DC, 3, D])
        wout = sb("wout", [P, DC, D])
        wg = sb("wg", [P, DC, E])
        part = sb("part", [P, 4, S], F32R)
        bcol = sb("bcol", [P, 2, 2])
        bv = sb("bv", [P, H, DH])
        bo = sb("bo", [P, D])
        ident = sb("ident", [P, P])
        ones = sb("ones", [P, P])
        upper = sb("upper", [P, P])
        mx = sb("mx", [P, 32])
        mT = sb("mT", [32, P], F32R)
        mzero = sb("mzero", [32, P])
        rs = sb("rs", [P, TPB, 4])
        flat = part[:].bitcast(F32).rearrange("p n s -> p (n s)")
        xn_p = flat[:, 0:TPB * D].rearrange("p (i d) -> p i d", d=D)
        yg = (flat[:, TPB * D:2 * TPB * D].rearrange("p (u k d) -> p u k d", u=2, k=2),
              flat.rearrange("p (u k d) -> p u k d", u=4, k=2))
        osb_flat = osb[:].rearrange("p n s -> p (n s)")
        xs = flat[:, 0:4 * D].rearrange("p (r d) -> p r d", r=4)
        hid = flat[:, 4 * D:4 * D + 2 * F].rearrange("p (r d) -> p r d", r=2)
        hidT = osb_flat[:, 0:2 * F].rearrange("p (r d) -> p r d", r=2)
        xsT = xT[:].rearrange("p c s -> p (c s)")[:, 0:2 * D].rearrange("p (r d) -> p r d", r=2)
        ysb = attn[:].rearrange("p a q n -> p (a q n)")[:, 0:4 * D].rearrange("p (r d) -> p r d", r=4)
        stats = sb("stats", [P, TPB, 6])
        mv = sb("mv", [P, TPB, 2])
        veps = sb("veps", [P, TPB])
        mhalf = sb("mhalf", [P, TPB])
        rstd = sb("rstd", [P, TPB])
        nmr = sb("nmr", [P, TPB])
        lg = sb("lg", [P, TPB, E])
        m8 = sb("m8", [P, TPB, 8])
        i8 = sb("i8", [P, TPB, 8], U32)
        i8f = sb("i8f", [P, TPB, 2])
        gap = sb("gap", [P, TPB])
        gexp = sb("gexp", [P, TPB])
        gden = sb("gden", [P, TPB])
        grec = sb("grec", [P, TPB])
        wts = sb("wts", [P, T, 2])
        oh = sb("oh", [P, T, 2, E])
        both = sb("both", [P, TPB, E])
        cum = sb("cum", [P, TPB + 1, E])
        rk = sb("rk", [P, T, E])
        rk_base = sb("rk_base", [P, TPB, E])
        pick = sb("pick", [P, TPB, 2, E])
        slot = sb("slot", [P, TPB, 2], U32)
        e_i = sb("e_i", [P, E], I32)
        e_f = sb("e_f", [P, E])
        e_base = sb("e_base", [P, E])
        j_f = sb("j_f", [P, TILES])
        cnt = sb("cnt", [P, E])
        cnt_i = sb("cnt_i", [P, E], I32)
        nt = sb("nt", [P, E])
        zero8 = sb("zero8", [P, E])
        ends = sb("ends", [P, E])
        start128 = sb("start128", [P, E])
        abase = sb("abase", [P, E])
        dbase = sb("dbase", [P, E])
        pad = sb("pad", [P, E], I32)
        exp_tab = sb("exp_tab", [P, TILES], I32)
        row_tab = sb("row_tab", [P, TILES], I32)
        yslot = sb("yslot", [P, T, 2], U32)
        yidx = sb("yidx", [P, 4, 2], U32)

        ps = ctx.enter_context(nc.psum_tensor("ps", [P, 8, 512], F32))
        O_BANK, T_BANK, M_BANK = 6, 7, 3

        def room(at, n):
            return flat[:, at:at + n]

        zrows = osb_flat[:, 3 * D:4 * D]
        rk_y = room(D, T * E).rearrange("p (t e) -> p t e", e=E)
        pick_y = room(2 * D, 2 * T * E).rearrange("p (t k e) -> p t k e", k=2, e=E)
        le = room(4 * D, TILES * E).rearrange("p (j e) -> p j e", e=E)
        lep = osb_flat[:, 0:TILES * E].rearrange("p (j e) -> p j e", e=E)
        ef, rowf, tmpj, j_scratch = (room(4 * D + TILES * (E + n), TILES) for n in range(4))
        j_i = j_scratch.bitcast(I32)
        wraw = vs[:].rearrange("p u t h w -> p (u t h w)")[:, 0:DC * 3 * D].rearrange("p (c n) -> p c n", c=DC)

        s_x = sem("x_loaded")
        s_w = sem("ffn_weights_loaded")
        s_wg = sem("gate_weights_loaded")
        s_small = sem("small_weights_loaded")
        s_sorted = sem("qkv_columns_sorted")
        s_iota = sem("iotas_made")
        s_const = sem("constants_made")
        s_dve0 = sem("dve_constants_made")

        class Norm:

            def __init__(self, n):
                self.stats = sem(n + "_stats")
                self.mv = sem(n + "_mean_var")
                self.veps = sem(n + "_var_eps")
                self.rstd = sem(n + "_rstd")
                self.nmr = sem(n + "_neg_mean_rstd")
                self.xn = sem(n + "_rows")
                self.tp = sem(n + "_transposed")
                self.ev0 = sem(n + "_chunk0_copied")
                self.ev1 = sem(n + "_chunk1_copied")

        class Route:

            def __init__(self, n, at):
                self.norm = Norm(n)
                self.lg_at, self.rank_at = at
                self.lg = sem(n + "_logits")
                self.d = sem(n + "_dve_step")
                self.gap = sem(n + "_gap_ready")
                self.exp = sem(n + "_gap_exp")
                self.cum = sem(n + "_counts_ready")
                self.rank = sem(n + "_ranks")
                self.slot = sem(n + "_slots")
                self.sent = sem(n + "_rows_sent")
                self.free = sem(n + "_rows_free")
                self.total = sem(n + "_totals")
                self.t = sem(n + "_table_step")
                self.tabs = sem(n + "_tables_ready")
                self.zero = sem(n + "_zero_rows")
                self.pad = sem(n + "_pads_sent")
                self.pad_ready = sem(n + "_pad_rows_ready")

        class Expert:

            def __init__(self, n):
                self.ld = [sem(f"{n}_rows_loaded{r}") for r in range(4)]
                self.tp = sem(n + "_rows_transposed")
                self.xT = sem(n + "_rowsT_copied")
                self.h = sem(n + "_hidden_made")
                self.relu = sem(n + "_hidden_relu")
                self.hTp = sem(n + "_hidden_transposed")
                self.hT = sem(n + "_hiddenT_copied")
                self.y = sem(n + "_y_made")
                self.ysb = sem(n + "_y_copied")
                self.st = [sem(f"{n}_y_stored{r}") for r in range(4)]

        r0 = Route("r0", at=((2, 0), (3, 0)))
        r1 = Route("r1", at=((7, 0), (7, 64)))
        npr = Norm("pr")
        x0, x1 = Expert("x0"), Expert("x1")
        s_gath = [[sem(f"gathered{l}_{r}") for r in range(2 + 2 * l)] for l in range(2)]
        s_idx = [sem(f"gather_rows{l}") for l in range(2)]
        s_comb = [sem(f"combined{l}") for l in range(2)]
        s_comb_half = [sem(f"combined_half{l}") for l in range(2)]
        s_qk = sem("qk_products")
        s_hi = sem("qk_hi")
        s_lo = sem("qk_lo")
        s_v = sem("v_products")
        s_vs = sem("v_copied")
        s_part = sem("parts_stored")
        s_ld = [sem(f"stack_loaded{c}") for c in range(2)]
        s_bias = sem("out_bias_added")
        s_mm = sem("max_scores")
        s_red = sem("max_reduced")
        s_mtr = sem("max_transposed")
        s_mev = sem("max_negated")
        s_mrow = [sem(f"max_row_placed{c}") for c in range(2)]
        s_sc = sem("scores")
        s_exp = sem("exps")
        s_pv = sem("pv")
        s_oev = sem("heads_copied")
        s_otr = sem("heads_transposed")
        s_rec = sem("sums_inverted")
        s_at = sem("heads_normalised")
        s_ptr = sem("attn_transposed")
        s_pev0 = sem("attnT0_copied")
        s_pev1 = sem("attnT1_copied")
        s_prj = sem("projected")
        s_x2 = sem("attention_added")
        s_out = sem("out_stored")

        NCONST = 8
        SMALL = 16 * (2 + 4 * HU + 2)

        block = ctx.enter_context(nc.Block())

        def apart(eng):
            eng.nop(nofuse=True)

        def dve_stats_tile(eng, n, b, i):
            apart(eng)
            nc.vector.bn_stats(stats[:, i, :], x[:, ds(b * TPB + i, 1), :].rearrange("p o d -> p (o d)")
                               ).then_inc(n.stats, 1)

        def dve_aggregate(eng, n, b):
            eng.wait_ge(n.stats, TPB * b + TPB)
            apart(eng)
            for i in range(TPB):
                nc.vector.bn_aggr(mv[:, i, :], stats[:, i, :]).then_inc(n.mv, 1)
            eng.wait_ge(n.mv, TPB * b + TPB)
            nc.vector.tensor_scalar(veps[:], mv[:, :, 1], 1e-5, None, ALU.add).then_inc(n.veps, 1)

        def dve_stats(eng, n, b):
            for i in range(TPB):
                dve_stats_tile(eng, n, b, i)
            dve_aggregate(eng, n, b)

        def dve_rows(eng, n, b, xn, xn_free=None):
            eng.wait_ge(n.rstd, b + 1)
            nc.vector.scalar_tensor_tensor(nmr[:], mv[:, :, 0], -1.0, rstd[:], ALU.mult, ALU.mult
                                           ).then_inc(n.nmr, 1)
            if xn_free is not None:
                xn_free()
            eng.wait_ge(n.nmr, b + 1)
            for i in range(TPB):
                nc.vector.tensor_scalar(xn[:, i, :], x[:, ds(b * TPB + i, 1), :].rearrange("p o d -> p (o d)"),
                                        rstd[:, i:i + 1], nmr[:, i:i + 1], ALU.mult, ALU.add
                                        ).then_inc(n.xn, 1)

        def dve_norm(eng, n, b, xn, xn_free=None):
            dve_stats(eng, n, b)
            dve_rows(eng, n, b, xn, xn_free)

        def pool_norm(eng, n, b):
            eng.wait_ge(n.veps, b + 1)
            nc.gpsimd.tensor_tensor(rstd[:], veps[:], mhalf[:], ALU.pow).then_inc(n.rstd, 1)

        def pe_norm(eng, n, b, xn, chunks=range(DC), banks=(0, 1)):
            eng.wait_ge(n.xn, TPB * b + TPB)
            for c in chunks:
                for i in range(TPB):
                    mm = nc.tensor.transpose(ps[:, banks[c], i * P:(i + 1) * P], xn[:, i, c * P:(c + 1) * P],
                                             ident[:])
                mm.then_inc(n.tp, 1)

        def act_norm(eng, n, b, bank=0):
            eng.wait_ge(n.tp, 2 * b + 1)
            nc.scalar.copy(xT[:, 0, :], ps[:, bank, :]).then_inc(n.ev0, 1)

        def dve_norm_copy(eng, n, b, bank=1):
            eng.wait_ge(n.tp, 2 * b + 2)
            nc.vector.tensor_copy(xT[:, 1, :], ps[:, bank, :]).then_inc(n.ev1, 1)

        def pe_logits(eng, r, b):
            eng.wait_ge(r.norm.ev0, b + 1)
            eng.wait_ge(r.norm.ev1, b + 1)
            bank, at = r.lg_at
            for i in range(TPB):
                for c in range(DC):
                    mm = nc.tensor.matmul(ps[:, bank, at + i * E:at + (i + 1) * E],
                                          xT[:, c, i * P:(i + 1) * P], wg[:, c, :],
                                          start=(c == 0), stop=(c == DC - 1))
            mm.then_inc(r.lg, 1)

        def pe_ranks(eng, r, b):
            eng.wait_ge(r.cum, TPB * b + TPB)
            bank, at = r.rank_at
            nc.tensor.matmul(ps[:, bank, at:at + G4], upper[:], both[:].rearrange("p i e -> p (i e)"),
                             start=True, stop=False)
            nc.tensor.matmul(ps[:, bank, at:at + G4], ones[:], cum[:, 0:TPB, :].rearrange("p i e -> p (i e)"),
                             start=False, stop=True).then_inc(r.rank, 1)

        def act_route(eng, r, b):
            eng.wait_ge(r.gap, b + 1)
            nc.scalar.activation(gexp[:], gap[:], ACT.Exp).then_inc(r.exp, 1)

        NSTEP = 2 * TPB + 6

        def dve_top2(eng, r, b):
            eng.wait_ge(r.lg, b + 1)
            base = NSTEP * b
            bank, at = r.lg_at
            nc.vector.tensor_copy(lg[:], ps[:, bank, at:at + G4].rearrange("p (i e) -> p i e", e=E)).then_inc(r.d, 1)
            eng.wait_ge(r.d, base + 1)
            apart(eng)
            for i in range(TPB):
                nc.vector.max(m8[:, i, :], lg[:, i, :]).then_inc(r.d, 1)
            eng.wait_ge(r.d, base + 1 + TPB)
            apart(eng)
            for i in range(TPB):
                nc.vector.max_index(i8[:, i, :], m8[:, i, :], lg[:, i, :]).then_inc(r.d, 1)
            nc.vector.tensor_tensor(gap[:], m8[:, :, 1], m8[:, :, 0], ALU.subtract).then_inc(r.gap, 1)

        def dve_onehots(eng, r, b):
            base = NSTEP * b
            eng.wait_ge(r.d, base + 1 + 2 * TPB)
            nc.vector.tensor_copy(i8f[:], i8[:, :, 0:2]).then_inc(r.d, 1)
            eng.wait_ge(r.d, base + 2 + 2 * TPB)
            ohb = oh[:, ds(b * TPB, TPB), :, :]
            nc.vector.tensor_tensor(
                ohb, i8f[:].unsqueeze(3).broadcast_to([P, TPB, 2, E]),
                e_f[:].unsqueeze(1).unsqueeze(1).broadcast_to([P, TPB, 2, E]), ALU.is_equal).then_inc(r.d, 1)
            eng.wait_ge(r.d, base + 3 + 2 * TPB)
            ohb0 = oh[:, ds(b * TPB, TPB), 0:1, :].rearrange("p i o e -> p i (o e)")
            ohb1 = oh[:, ds(b * TPB, TPB), 1:2, :].rearrange("p i o e -> p i (o e)")
            nc.vector.tensor_tensor(both[:], ohb0, ohb1, ALU.add).then_inc(r.d, 1)

        def dve_counts(eng, r, b):
            base = NSTEP * b
            eng.wait_ge(r.d, base + 4 + 2 * TPB)
            for i in range(TPB):
                nc.vector.tensor_tensor(cum[:, i + 1, :], cum[:, i, :], both[:, i, :], ALU.add).then_inc(r.cum, 1)
                eng.wait_ge(r.cum, TPB * b + i + 1)

        def dve_weights(eng, r, b):
            base = NSTEP * b
            eng.wait_ge(r.exp, b + 1)
            nc.vector.tensor_scalar(gden[:], gexp[:], 2.0, 2.0, ALU.mult, ALU.add).then_inc(r.d, 1)
            eng.wait_ge(r.d, base + 5 + 2 * TPB)
            nc.vector.reciprocal(grec[:], gden[:]).then_inc(r.d, 1)
            eng.wait_ge(r.d, base + 6 + 2 * TPB)
            apart(eng)
            nc.vector.tensor_copy(wts[:, ds(b * TPB, TPB), 0:1], grec[:].unsqueeze(2))
            nc.vector.tensor_tensor(wts[:, ds(b * TPB, TPB), 1:2], grec[:].unsqueeze(2), gexp[:].unsqueeze(2),
                                    ALU.mult).then_inc(r.slot, 1)

        def dve_slots(eng, r, b):
            ohb = oh[:, ds(b * TPB, TPB), :, :]
            eng.wait_ge(r.rank, b + 1)
            apart(eng)
            bank, at = r.rank_at
            rkv = ps[:, bank, at:at + G4].rearrange("p (i e) -> p i e", e=E)
            nc.vector.tensor_copy(rk[:, ds(b * TPB, TPB), :], rkv).then_inc(r.slot, 1)
            nc.vector.tensor_tensor(rk_base[:], rkv, e_base[:].unsqueeze(1).broadcast_to([P, TPB, E]), ALU.add
                                    ).then_inc(r.slot, 1)
            nc.vector.tensor_copy(cum[:, 0, :], cum[:, TPB, :]).then_inc(r.slot, 1)
            eng.wait_ge(r.slot, 6 * b + 4)
            nc.vector.tensor_tensor(pick[:], ohb, rk_base[:].unsqueeze(2).broadcast_to([P, TPB, 2, E]), ALU.mult
                                    ).then_inc(r.slot, 1)
            eng.wait_ge(r.slot, 6 * b + 5)
            if live_b(b, 1):
                if r is r0:
                    eng.wait_ge(r.sent, SENT * b)
                else:
                    eng.wait_ge(r.free, b + 1)
            with nc.allow_low_precision(reason="row numbers below 2**24, exact in float32"):
                nc.vector.tensor_reduce(slot[:], pick[:], AXX, ALU.add).then_inc(r.slot, 1)

        def pool_send(eng, r, b, xn):
            eng.wait_ge(r.slot, 6 * b + 6)
            apart(eng)
            for i in range(TPB):
                for k in range(2):
                    nc.gpsimd.indirect_dma_start(
                        out=xs_dram[:, :],
                        out_offset=bass.IndirectOffsetOnAxis(
                            ap=slot[:, i, k:k + 1], axis=0),
                        in_=xn[:, i, :], in_offset=None).then_inc(r.sent, 16)

        SENT = 16 * 2 * TPB

        def pe_total(eng, r):
            eng.wait_ge(r.cum, TPB * B)
            eng.wait_ge(r.slot, 6 * B)
            nc.tensor.matmul(ps[:, 2, 0:E], ones[:], cum[:, TPB, :], start=True, stop=True).then_inc(r.total, 1)

        def dve_tables(eng, r):
            n = [0]

            def step(ins):
                ins.then_inc(r.t, 1)
                n[0] += 1
                eng.wait_ge(r.t, n[0])

            eng.wait_ge(r.total, 1)
            step(nc.vector.tensor_copy(cnt[:], ps[:, 2, 0:E]))
            nc.vector.tensor_tensor(pad[:], cnt[:], e_base[:], ALU.add).then_inc(r.pad_ready, 1)
            nc.vector.memset(zrows, 0.0).then_inc(r.zero, 1)
            step(nc.vector.tensor_scalar(cnt_i[:], cnt[:], float(P - 1), None, ALU.add))
            step(nc.vector.tensor_scalar(cnt_i[:], cnt_i[:], 7, None, ALU.arith_shift_right))
            step(nc.vector.tensor_copy(nt[:], cnt_i[:]))
            step(nc.vector.tensor_tensor_scan(ends[:], nt[:], zero8[:], 0.0, ALU.add, ALU.add))
            step(nc.vector.tensor_tensor(start128[:], ends[:], nt[:], ALU.subtract))
            step(nc.vector.tensor_scalar(start128[:], start128[:], float(P), None, ALU.mult))
            step(nc.vector.tensor_tensor(abase[:], e_base[:], start128[:], ALU.subtract))
            step(nc.vector.memset(dbase[:], 0.0))
            step(nc.vector.tensor_tensor(dbase[:, 0:E - 1], abase[:, 1:E], abase[:, 0:E - 1], ALU.subtract))
            step(nc.vector.tensor_tensor(le[:], ends[:].unsqueeze(1).broadcast_to([P, TILES, E]),
                                         j_f[:].unsqueeze(2).broadcast_to([P, TILES, E]), ALU.is_le))
            step(nc.vector.tensor_reduce(ef[:], le[:], AXX, ALU.add))
            step(nc.vector.tensor_scalar(exp_tab[:], ef[:], float(E - 1), None, ALU.min))
            step(nc.vector.tensor_tensor(lep, le[:], dbase[:].unsqueeze(1).broadcast_to([P, TILES, E]), ALU.mult))
            step(nc.vector.tensor_reduce(tmpj[:], lep, AXX, ALU.add))
            step(nc.vector.scalar_tensor_tensor(rowf[:], j_f[:], float(P), tmpj[:], ALU.mult, ALU.add))
            step(nc.vector.tensor_scalar(tmpj[:], rowf[:], -1.0, float((E - 1) * REGION), ALU.mult, ALU.add))
            step(nc.vector.tensor_tensor(tmpj[:], tmpj[:], le[:, :, E - 1], ALU.mult))
            step(nc.vector.tensor_tensor(row_tab[:], rowf[:], tmpj[:], ALU.add))
            eng.wait_ge(r.sent, SENT * B)
            step(nc.vector.tensor_tensor(rk_y, rk[:], start128[:].unsqueeze(1).broadcast_to([P, T, E]), ALU.add))
            step(nc.vector.tensor_tensor(pick_y, oh[:], rk_y.unsqueeze(2).broadcast_to([P, T, 2, E]), ALU.mult))
            with nc.allow_low_precision(reason="row numbers below 2**24, exact in float32"):
                nc.vector.tensor_reduce(yslot[:], pick_y, AXX, ALU.add).then_inc(r.tabs, 1)
            nc.vector.memset(cum[:, 0, :], 0.0).then_inc(r.tabs, 1)
            eng.wait_ge(r.tabs, 2)

        def sp_pads(eng, r):
            eng.wait_ge(r.pad_ready, 1)
            eng.wait_ge(r.zero, 1)
            for e in range(E):
                row = eng.value_load(pad[0:1, e:e + 1], min_val=0, max_val=E * REGION - P)
                eng.dma_start(xs_dram[ds(row, P), :], zrows).then_inc(r.pad, 16)
            eng.wait_ge(r.pad, 16 * E)
            eng.wait_ge(r.sent, SENT * B)

        def expert_engines(q, r):
            STEPS = TILES + 6

            def steps(eng, body):
                for i in range(8):
                    body(i, i % 4)
                with eng.Fori(2, TILES // 4) as it:
                    for u in range(4):
                        body(it * 4 + u, u)
                for i in range(TILES, STEPS):
                    body(i, i % 4)

            def live(i, k):
                return not isinstance(i, int) or 0 <= i - k < TILES

            def ge(eng, s, v):
                if not isinstance(v, int) or v > 0:
                    eng.wait_ge(s, v)

            def turns(i, u, back):
                if isinstance(i, int):
                    return 16 * ((i - back) // 4 + 1)
                return (i - u) * 4 + 16 * ((u - back) // 4 + 1)

            def sp(eng):
                sp_pads(eng, r)
                eng.wait_ge(r.tabs, 1)

                def body(i, u):
                    if live(i, 0):
                        ge(eng, q.tp, i - 3)
                        apart(eng)
                        row = eng.value_load(row_tab[0:1, ds(i, 1)], min_val=0, max_val=E * REGION - P)
                        eng.dma_start(xs[:, u, :], xs_dram[ds(row, P), :]).then_inc(q.ld[u], 16)
                    if live(i, 6):
                        ge(eng, q.ysb, i - 5)
                        w = (u - 6) % 4
                        apart(eng)
                        eng.dma_start(y_dram[ds((i - 6) * P, P), :], ysb[:, w, :]).then_inc(q.st[w], 16)
                steps(eng, body)
                for w in range(4):
                    eng.wait_ge(q.st[w], 16 * (TILES // 4))

            def pe(eng):
                eng.wait_ge(r.tabs, 1)
                eng.wait_ge(s_w, 32 * E if q is x0 else 48 * E)

                def weights_of(tile):
                    return eng.value_load(exp_tab[0:1, ds(tile, 1)], min_val=0, max_val=E - 1)

                def body(i, u):
                    if live(i, 0):
                        ge(eng, q.xT, i - 1)
                        eng.wait_ge(q.ld[u], turns(i, u, 0))
                        for c in range(DC):
                            mm = nc.tensor.transpose(ps[:, u % 2, c * P:(c + 1) * P],
                                                     xs[:, u, c * P:(c + 1) * P], ident[:])
                        mm.then_inc(q.tp, 1)
                    if live(i, 1):
                        e = weights_of(i - 1)
                        w = (u + 1) % 2
                        ge(eng, q.xT, i)
                        ge(eng, q.relu, i - 2)
                        for c in range(DC):
                            mm = nc.tensor.matmul(ps[:, 2 + w, :], xsT[:, w, c * P:(c + 1) * P],
                                                  w1s[:, ds(e, 1), c:c + 1, :].rearrange("p a b f -> p (a b f)"),
                                                  start=(c == 0), stop=(c == DC - 1))
                        mm.then_inc(q.h, 1)
                    if live(i, 2):
                        w = u % 2
                        ge(eng, q.relu, i - 1)
                        ge(eng, q.hT, i - 3)
                        for c in range(FC):
                            mm = nc.tensor.transpose(ps[:, 4 + w, c * P:(c + 1) * P],
                                                     hid[:, w, c * P:(c + 1) * P], ident[:])
                        mm.then_inc(q.hTp, 1)
                    if live(i, 3):
                        e = weights_of(i - 3)
                        w = (u + 1) % 2
                        ge(eng, q.hT, i - 2)
                        ge(eng, q.ysb, i - 4)
                        for c in range(FC):
                            mm = nc.tensor.matmul(ps[:, 6 + w, 0:D], hidT[:, w, c * P:(c + 1) * P],
                                                  w2s[:, ds(e, 1), c:c + 1, :].rearrange("p a b f -> p (a b f)"),
                                                  start=(c == 0), stop=(c == FC - 1))
                        mm.then_inc(q.y, 1)
                steps(eng, body)

            def act(eng):
                def body(i, u):
                    if live(i, 0):
                        eng.wait_ge(q.tp, i + 1)
                        ge(eng, q.h, i - 1)
                        nc.scalar.copy(xsT[:, u % 2, :], ps[:, u % 2, 0:D]).then_inc(q.xT, 1)
                    if live(i, 1):
                        w = (u + 1) % 2
                        ge(eng, q.h, i)
                        ge(eng, q.hTp, i - 2)
                        nc.scalar.activation(hid[:, w, :], ps[:, 2 + w, :], ACT.Relu).then_inc(q.relu, 1)
                steps(eng, body)

            def dve(eng):
                def body(i, u):
                    if live(i, 2):
                        w = u % 2
                        ge(eng, q.hTp, i - 1)
                        ge(eng, q.y, i - 3)
                        nc.vector.tensor_copy(hidT[:, w, :], ps[:, 4 + w, :]).then_inc(q.hT, 1)
                    if live(i, 3):
                        w, v = (u + 1) % 2, (u + 1) % 4
                        ge(eng, q.y, i - 2)
                        if not isinstance(i, int) or i >= 7:
                            eng.wait_ge(q.st[v], turns(i, u, 7))
                        nc.vector.tensor_copy(ysb[:, v, :], ps[:, 6 + w, 0:D]).then_inc(q.ysb, 1)
                steps(eng, body)

            return sp, pe, act, dve

        e0, e1 = expert_engines(x0, r0), expert_engines(x1, r1)

        def pool_gather(eng, l, t, u):
            ring = 2 + 2 * l
            if not isinstance(t, int) or t >= ring:
                eng.wait_ge(s_comb[l], t - ring + 1)
            nc.gpsimd.tensor_copy(yidx[:, u:u + 1, :], yslot[:, ds(t, 1), :]).then_inc(s_idx[l], 1)
            eng.wait_ge(s_idx[l], t + 1)
            apart(eng)
            for k in range(2):
                nc.gpsimd.indirect_dma_start(
                    out=yg[l][:, u, k, :], out_offset=None, in_=y_dram[:, :],
                    in_offset=bass.IndirectOffsetOnAxis(
                        ap=yidx[:, u, k:k + 1], axis=0)
                ).then_inc(s_gath[l][u], 16)

        def dve_combine(eng, l, t, u, turn):
            eng.wait_ge(s_gath[l][u], turn * 32 + 32)
            xt = x[:, ds(t, 1), :].rearrange("p o d -> p (o d)")
            w = wts[:, ds(t, 1), :].rearrange("p o k -> p (o k)")
            nc.vector.scalar_tensor_tensor(xt, yg[l][:, u, 0, :], w[:, 0:1], xt, ALU.mult, ALU.add
                                           ).then_inc(s_comb_half[l], 1)
            eng.wait_ge(s_comb_half[l], t + 1)
            nc.vector.scalar_tensor_tensor(xt, yg[l][:, u, 1, :], w[:, 1:2], xt, ALU.mult, ALU.add
                                           ).then_inc(s_comb[l], 1)

        def pool_early(eng, b):
            if live_b(b, 1):
                eng.wait_ge(s_part, 128 * b)
            for i in range(TPB):
                pool_gather(eng, 0, b * TPB + i, i % 2)
            pool_norm(eng, npr, b)
            eng.wait_ge(npr.xn, TPB * b + TPB)
            xb = x[:, ds(b * TPB, TPB), :]
            nc.gpsimd.tensor_tensor(xb, xb, bo[:].unsqueeze(1).broadcast_to([P, TPB, D]), ALU.add
                                    ).then_inc(s_bias, 1)

        def dve_early_stats(eng, b):
            eng.wait_ge(s_comb[0], b * TPB + TPB)
            dve_stats(eng, npr, b)

        def dve_early_rows(eng, b):
            def free():
                if live_b(b, 1):
                    eng.wait_ge(s_part, 128 * b)
                if live_b(b, 2):
                    eng.wait_ge(r1.free, b - 1)
            dve_rows(eng, npr, b, xn_p, free)

        def dve_prep(eng, b, bb):
            dve_norm_copy(eng, npr, b)
            if bb is not None:
                dve_normalise(eng, 4 * bb + 3, 1, 1)
            for c in range(2):
                for n in range(2):
                    eng.wait_ge(s_hi, 4 * b + 2 * c + n + 1)
                    nc.vector.scalar_tensor_tensor(
                        part[:, 2 * n + 1, :], ps[:, n, :], bcol[:, c, n:n + 1],
                        part[:, 2 * n, :].bitcast(F32), ALU.add, ALU.subtract).then_inc(s_lo, 1)
                eng.wait_ge(s_v, 2 * b + c + 1)
                nc.vector.tensor_tensor(
                    vs[:, vbuf(b), 2 * c:2 * c + 2, :, 0:DH],
                    ps[:, 2 + c, :].rearrange("p (i h d) -> p i h d", i=2, h=H),
                    bv[:].unsqueeze(1).broadcast_to([P, 2, H, DH]), ALU.add).then_inc(s_vs, 1)
                if c == 0 and bb is not None:
                    dve_attnT(eng, bb)

        def act_prep(eng, b, bb):
            act_norm(eng, npr, b)
            for c in range(2):
                if c == 1 and bb is not None:
                    act_attnT(eng, bb)
                for n in range(2):
                    eng.wait_ge(s_qk, 4 * b + 2 * c + n + 1)
                    if n == 0 and (c or live_b(b, 1)):
                        eng.wait_ge(s_part, 64 * (2 * b + c))
                    nc.scalar.activation(part[:, 2 * n, :], ps[:, n, :], ACT.Identity, bias=bcol[:, c, n:n + 1]
                                         ).then_inc(s_hi, 1)

        def pe_prep(eng, b, bb):
            if live_b(b, 1):
                eng.wait_ge(s_red, 16 * (2 * b - 1))
            pe_norm(eng, npr, b, xn_p)
            if bb is not None:
                eng.wait_ge(s_at, 4 * bb + 3)
                pe_heads(eng, 4 * bb + 3, 1)
            eng.wait_ge(npr.ev0, b + 1)
            eng.wait_ge(npr.ev1, b + 1)
            for c in range(2):
                if c and bb is not None:
                    pe_attnT(eng, bb)
                for n in range(2):
                    if c:
                        eng.wait_ge(s_lo, 4 * b + n + 1)
                    for k in range(DC):
                        mm = nc.tensor.matmul(ps[:, n, :], wqkv[:, k, n, P * c:P * c + P], xT[:, k, :],
                                              start=(k == 0), stop=(k == DC - 1))
                    mm.then_inc(s_qk, 1)
                if c and live_b(b, 1):
                    eng.wait_ge(s_mev, 2 * b - 1)
                for i in range(2 * c, 2 * c + 2):
                    o = ps[:, 2 + i // 2, (i % 2) * D:(i % 2) * D + D]
                    for k in range(DC):
                        mm = nc.tensor.matmul(o, xT[:, k, i * P:(i + 1) * P], wqkv[:, k, 2, :],
                                              start=(k == 0), stop=(k == DC - 1))
                mm.then_inc(s_v, 1)

        LOADS = 16 * 14

        def sp_parts(eng, b, c):
            if live_b(b, 1):
                eng.wait_ge(s_ld[c], LOADS * b)
                apart(eng)
            for n in range(2):
                eng.wait_ge(s_hi, 4 * b + 2 * c + n + 1)
                eng.dma_start(qk_dram[c, 2 * n], part[:, 2 * n, :].bitcast(F32)).then_inc(s_part, 16)
                eng.wait_ge(s_lo, 4 * b + 2 * c + n + 1)
                eng.dma_start(qk_dram[c, 2 * n + 1], part[:, 2 * n + 1, :].bitcast(F32)).then_inc(s_part, 16)
            eng.wait_ge(s_part, 64 * (2 * b + c + 1))

        def sp_stack(eng, b, c, u3):
            if not isinstance(b, int) or 2 * b + c >= 3:
                eng.wait_ge(s_sc, 32 * (2 * b + c - 2))
            k_by_parity = kst[:].rearrange("p u (g r) s -> p u r g s", r=2)
            rows = [(qst, 0, 0), (qst, 1, 0), (qst, 2, 1), (kst, 0, 2), (kst, 1, 3), (kst, 2, 2)]
            for dst, row, src in rows:
                for par in range(2):
                    p0 = 64 * par + DH * row
                    to = qst[p0:p0 + DH, u3] if dst is qst else k_by_parity[p0:p0 + DH, u3, par]
                    eng.dma_start(to.bitcast(F32),
                                  qk_dram[c, src].rearrange("(g r d) n -> r d g n", r=2, d=DH)[par]
                                  ).then_inc(s_ld[c], 16)
            for par in range(2):
                r = 64 * par + 3 * DH
                eng.dma_start(qst[r:r + 1, u3, :, :].bitcast(F32), mzero[0:16, :]).then_inc(s_ld[c], 16)

        def live_b(b, n):
            return b >= n if isinstance(b, int) else True

        def pe_max_tile(b, c, u3, s):
            pair, par, qt = s // 8, s % 2, (s % 8) // 2
            return nc.tensor.matmul(ps[:, s % 4, :], qst[:, u3, pair, qt * P:(qt + 1) * P],
                                    kst[:, u3, 2 * pair + par, :], start=True, stop=True)

        def pe_pv(eng, b, c, m):
            g, kt = m // 4, m % 4
            U8 = 8 * (2 * b + c)
            eng.wait_ge(s_exp, 4 * (U8 + m) + 4)
            if kt == 0 and (g or c or live_b(b, 1)):
                eng.wait_ge(s_oev, 2 * (2 * b + c) + g)
            for hh in range(4):
                h = c * HU + 4 * g + hh
                mm = nc.tensor.matmul(ps[32 * hh:32 * hh + VW, O_BANK, :], vs[:, vbuf(b), kt, h, :],
                                      probs[:, (4 * m + hh) % 16, :], start=(kt == 0), stop=(kt == 3))
            mm.then_inc(s_pv, 1)

        def pe_heads(eng, n, slot_):
            eng.wait_ge(s_oev, n + 1)
            for qt in range(TPB):
                mm = nc.tensor.transpose(ps[:, T_BANK, qt * P:(qt + 1) * P], osb[:, slot_, qt * P:(qt + 1) * P],
                                         ident[:])
            mm.then_inc(s_otr, 1)

        LEAD = 3
        PV_STEPS = (10, 18, 26)

        def pe_unit(eng, b, c, nxt, routed=None):
            U = None if b is None else 2 * b + c
            if nxt is not None:
                nb, ncx, nu4 = nxt
                NU = 2 * nb + ncx
                eng.wait_ge(s_ld[ncx], LOADS * nb + LOADS)

            def maxima(t):
                if nxt is None or t >= 32:
                    return
                if t % 2 == 0 and (t >= 4 or ncx or live_b(nb, 1)):
                    eng.wait_ge(s_red, 16 * NU + t // 2 - 1)
                if t == 3 and (ncx or live_b(nb, 1)):
                    eng.wait_ge(s_mev, NU)
                mm = pe_max_tile(nb, ncx, nu4, t)
                if t % 2 == 1:
                    mm.then_inc(s_mm, 1)

            for t in range(LEAD):
                maxima(t)
            if b is not None:
                eng.wait_ge(s_mrow[c], 32 * b + 32)
                if c == 0:
                    eng.wait_ge(s_vs, 2 * b + 2)
                    if not (isinstance(b, int) and b == 0):
                        eng.wait_ge(s_x2, 2 * b)
            for s in range(32):
                maxima(s + LEAD)
                if b is None:
                    continue
                if s >= 2 or c or live_b(b, 1):
                    eng.wait_ge(s_exp, 32 * U + s - 1)
                g, kt, hh = s // 16, (s % 16) // 4, s % 4
                pair, par = 2 * g + hh // 2, hh % 2
                nc.tensor.matmul(ps[:, 4 + s % 2, :], kst[:, ubuf(b, c), 2 * pair + par, kt * P:(kt + 1) * P],
                                 qst[:, ubuf(b, c), pair, :], start=True, stop=True).then_inc(s_sc, 1)
                if s in PV_STEPS:
                    pe_pv(eng, b, c, s // 4 - 2)
                    pe_pv(eng, b, c, s // 4 - 1)
                if s == 14 and c:
                    eng.wait_ge(s_at, 2 * U - 1)
                    pe_heads(eng, 2 * U - 1, 1)
                if routed is not None:
                    if s == 13:
                        eng.wait_ge(s_at, 2 * U)
                        pe_norm(eng, r1.norm, routed, xn_p, chunks=(0,), banks=(7, 7))
                    if s == 16:
                        eng.wait_ge(r1.norm.ev0, routed + 1)
                        pe_norm(eng, r1.norm, routed, xn_p, chunks=(1,), banks=(7, 7))
                    if s == 20:
                        pe_logits(eng, r1, routed)
                    if s == 27:
                        pe_ranks(eng, r1, routed)
                if s == 30:
                    if routed is not None:
                        eng.wait_ge(r1.slot, 6 * routed + 4)
                    if c or live_b(b, 1):
                        eng.wait_ge(s_at, 2 * U)
                    pe_heads(eng, 2 * U, 0)
            if nxt is not None:
                eng.wait_ge(s_red, 16 * NU + 16)
                nc.tensor.transpose(ps[0:32, M_BANK, 0:P], mx[:], ident[:]).then_inc(s_mtr, 1)
            if b is not None:
                for m in (6, 7):
                    pe_pv(eng, b, c, m)

        def act_unit(eng, b, c, nxt, routed=None):
            U = None if b is None else 2 * b + c

            def heads_copy(g):
                eng.wait_ge(s_pv, 8 * U + 4 * g + 4)
                if not (isinstance(U, int) and 2 * U + g < 2):
                    eng.wait_ge(s_otr, 2 * U + g - 1)
                nc.scalar.copy(osb[:, g, :], ps[:, O_BANK, :]).then_inc(s_oev, 1)

            if b is not None:
                for s in range(32):
                    eng.wait_ge(s_sc, 32 * U + s + 1)
                    if s >= 16 or c or live_b(b, 1):
                        eng.wait_ge(s_pv, 8 * U + s // 4 - 3)
                    nc.scalar.activation(probs[:, s % 16, :], ps[:, 4 + s % 2, :], ACT.Exp, scale=LOGIT_SCALE
                                         ).then_inc(s_exp, 1)
                    if s == 24:
                        heads_copy(0)
                    if routed is not None and s == 14:
                        act_norm(eng, r1.norm, routed, bank=7)
                    if routed is not None and s == 24:
                        act_route(eng, r1, routed)
            if nxt is not None:
                nb, ncx, nu4 = nxt
                NU = 2 * nb + ncx
                eng.wait_ge(s_mtr, NU + 1)
                if live_b(nb, 1) or ncx:
                    if ncx:
                        eng.wait_ge(s_mrow[0], 32 * nb + 32)
                    else:
                        eng.wait_ge(s_mrow[1], 32 * nb)
                nc.scalar.activation(mT[:], ps[0:32, M_BANK, 0:P], ACT.Copy, scale=-1.0).then_inc(s_mev, 1)
                eng.wait_ge(s_mev, NU + 1)
                for par in range(2):
                    r = 64 * par + 3 * DH
                    eng.dma_start(qst[r:r + 1, nu4, :, :].bitcast(F32), mT[16 * par:16 * par + 16, :].bitcast(F32)
                                  ).then_inc(s_mrow[ncx], 16)
            if b is not None:
                heads_copy(1)

        def dve_normalise(eng, n, c, g):
            eng.wait_ge(s_otr, n + 1)
            o = ps[:, T_BANK, :].rearrange("p (q h w) -> p q h w", q=TPB, h=4)
            if not (isinstance(n, int) and n == 0):
                eng.wait_ge(s_at, n)
            nc.vector.reciprocal(rs[:].unsqueeze(3), o[:, :, :, DH:DH + 1]).then_inc(s_rec, 1)
            eng.wait_ge(s_rec, n + 1)
            dst = attn[:, c, :, 64 * g:64 * g + 64].rearrange("p q (h d) -> p q h d", h=4)
            nc.vector.tensor_tensor(dst, o[:, :, :, 0:DH], rs[:].unsqueeze(3).broadcast_to([P, TPB, 4, DH]),
                                    ALU.mult).then_inc(s_at, 1)

        def dve_unit(eng, b, c, nxt, routed=None, early=None):
            U = None if b is None else 2 * b + c
            for j in range(16):
                if nxt is not None:
                    nb, ncx, nu4 = nxt
                    NU = 2 * nb + ncx
                    if j == 0 and (ncx or live_b(nb, 1)):
                        eng.wait_ge(s_mtr, NU)
                    eng.wait_ge(s_mm, 16 * NU + j + 1)
                    dst = mx[:].rearrange("p (r c) -> p r c", r=2)[:, :, j:j + 1]
                    bk = (2 * j) % 4
                    nc.vector.tensor_reduce(dst, ps[:, bk:bk + 2, :].unsqueeze(2), AXX, ALU.max
                                            ).then_inc(s_red, 1)
                if early is not None:
                    if j in (7, 8, 11, 12):
                        i = (7, 8, 11, 12).index(j)
                        dve_combine(eng, 0, early * TPB + i, i % 2, early * 2 + i // 2)
                    if j in (9, 10, 13, 14):
                        i = (9, 10, 13, 14).index(j)
                        if i % 2 == 0:
                            eng.wait_ge(s_comb[0], early * TPB + i + 2)
                        dve_stats_tile(eng, npr, early, i)
                    if j == 15:
                        dve_aggregate(eng, npr, early)
                if routed is not None:
                    if j < 4:
                        dve_stats_tile(eng, r1.norm, routed, j)
                    if j == 4:
                        dve_aggregate(eng, r1.norm, routed)
                    if j == 5:
                        dve_rows(eng, r1.norm, routed, xn_p, lambda: eng.wait_ge(
                            s_part, min(128 * B, 128 * (routed + 3)) if isinstance(routed, int)
                            else 128 * (routed + 3)))
                    if j == 9:
                        dve_norm_copy(eng, r1.norm, routed, bank=7)
                    if j == 11:
                        dve_top2(eng, r1, routed)
                    if j == 12:
                        dve_onehots(eng, r1, routed)
                    if j == 13:
                        dve_counts(eng, r1, routed)
                        dve_weights(eng, r1, routed)
                    if j == 14:
                        dve_slots(eng, r1, routed)
                if b is None:
                    continue
                if j == 8 and c:
                    dve_normalise(eng, 2 * U - 1, 0, 1)
                if j == 15:
                    dve_normalise(eng, 2 * U, c, 0)
            if early is not None:
                dve_early_rows(eng, early)

        def pe_attnT(eng, b):
            eng.wait_ge(s_at, 4 * b + 4)
            for c in range(DC):
                for qt in range(TPB):
                    mm = nc.tensor.transpose(ps[:, 4 + c, qt * P:(qt + 1) * P], attn[:, c, qt, :], ident[:])
                mm.then_inc(s_ptr, 1)

        def act_attnT(eng, b):
            eng.wait_ge(s_ptr, 2 * b + 1)
            nc.scalar.copy(osb[:, 0, :], ps[:, 4, :]).then_inc(s_pev0, 1)

        def dve_attnT(eng, b):
            eng.wait_ge(s_ptr, 2 * b + 2)
            nc.vector.tensor_copy(osb[:, 1, :], ps[:, 5, :]).then_inc(s_pev1, 1)

        def pe_project(eng, b):
            eng.wait_ge(s_pev0, b + 1)
            eng.wait_ge(s_pev1, b + 1)
            for i in range(TPB):
                o = ps[:, 4 + i // 2, (i % 2) * D:(i % 2) * D + D]
                for k in range(DC):
                    mm = nc.tensor.matmul(o, osb[:, k, i * P:(i + 1) * P], wout[:, k, :],
                                          start=(k == 0), stop=(k == DC - 1))
                if i % 2:
                    mm.then_inc(s_prj, 1)

        def dve_project(eng, b):
            eng.wait_ge(s_bias, b + 1)
            for j in range(2):
                eng.wait_ge(s_prj, 2 * b + j + 1)
                xb = x[:, ds(b * TPB + 2 * j, 2), :]
                nc.vector.tensor_tensor(xb, ps[:, 4 + j, :].rearrange("p (i d) -> p i d", i=2), xb, ALU.add
                                        ).then_inc(s_x2, 1)
            eng.wait_ge(s_x2, 2 * b + 2)

        def pool_post(eng, b):
            pool_norm(eng, r1.norm, b)
            pool_send(eng, r1, b, xn_p)
            eng.wait_ge(r1.sent, SENT * b + SENT)
            eng.sem_inc(r1.free, 1)

        modulo = {}

        def vbuf(b):
            return b % 3 if isinstance(b, int) else modulo[id(b)]

        def ubuf(b, c):
            return (2 * vbuf(b) + c) % 3

        kept = []

        def attention(eng, prep, unit, project):
            def turn(b, before, after):
                unit(before, 1, (b, 0, ubuf(b, 0)), None, after)
                if after is not None:
                    prep(after, before)
                project(before, after)
                unit(b, 0, (b, 1, ubuf(b, 1)), before, None)

            prep(0, None)
            unit(None, 0, (0, 0, ubuf(0, 0)), None, 1)
            prep(1, None)
            unit(0, 0, (0, 1, ubuf(0, 1)), None, None)
            with eng.Fori(0, (B - 2) // 3) as it:
                for j in range(3):
                    numbers = [it * 3 + (1 + j + d) if 1 + j + d else it * 3 for d in (0, -1, 1)]
                    for v, d in zip(numbers, (0, -1, 1)):
                        modulo[id(v)] = (1 + j + d) % 3
                    kept.append(numbers)
                    turn(*numbers)
            turn(B - 1, B - 2, None)
            unit(B - 1, 1, None, None, None)
            project(B - 1, None)

        def route0(eng, turn):
            turn(0, 0, True)
            with eng.Fori(0, (B - 2) // 2) as it:
                turn(it * 2 + 1, 1, True)
                turn(it * 2 + 2, 0, True)
            turn(B - 1, (B - 1) % 2, False)

        xn0 = (xn_p, attn[:].rearrange("p a q n -> p (a q n)")[:, 0:TPB * D].rearrange("p (i d) -> p i d", d=D))

        def dve_route0(eng, g, par, more):
            if more:
                eng.wait_ge(s_x, g * 16 + 32)
                dve_stats(eng, r0.norm, g + 1)
            for stage in (dve_top2, dve_onehots, dve_counts, dve_weights):
                stage(eng, r0, g)
            if more:
                dve_rows(eng, r0.norm, g + 1, xn0[1 - par],
                         (lambda: eng.wait_ge(r0.sent, SENT * g)) if live_b(g, 1) else None)
            dve_slots(eng, r0, g)
            if more:
                dve_norm_copy(eng, r0.norm, g + 1)

        def pool_route0(eng, g, par, more):
            if more:
                pool_norm(eng, r0.norm, g + 1)
            pool_send(eng, r0, g, xn0[par])

        def act_route0(eng, g, par, more):
            act_route(eng, r0, g)
            if more:
                act_norm(eng, r0.norm, g + 1)

        def pe_route0(eng, g, par, more):
            if live_b(g, 1):
                eng.wait_ge(r0.slot, 6 * g)
            pe_ranks(eng, r0, g)
            if more:
                pe_norm(eng, r0.norm, g + 1, xn0[1 - par])
                pe_logits(eng, r0, g + 1)

        @block.sync
        def _(eng):
            with eng.Fori(0, B) as g:
                eng.dma_start(x[:, ds(g * TPB, TPB), :], x_tok[:, ds(g * TPB, TPB), :]).then_inc(s_x, 16)
                eng.wait_ge(s_x, g * 16 + 16)
                apart(eng)
            with nc.allow_non_contiguous_dma(reason="bias columns"):
                eng.dma_start(wraw,
                              w_qkv.rearrange("(c p) n -> p c n", p=P)).then_inc(s_small, 16)
                eng.dma_start(wout[:], w_out.rearrange("(c p) n -> p c n", p=P)).then_inc(s_small, 16)
                bq = b_qkv.rearrange("(c h n d) -> n c h d", c=2, n=3, d=DH)
                for n in range(2):
                    for c in range(2):
                        for h in range(HU):
                            eng.dma_start(bcol[DH * h:DH * h + DH, c, n:n + 1],
                                          bq[n, c, h].unsqueeze(1)).then_inc(s_small, 16)
                eng.dma_start(bv[:], b_qkv.rearrange("(o h n d) -> n o h d", o=1, n=3, d=DH)[2]
                              .broadcast_to([P, H, DH])).then_inc(s_small, 16)
                eng.dma_start(bo[:], b_out.rearrange("(o d) -> o d", o=1).broadcast_to([P, D])
                              ).then_inc(s_small, 16)
            w1_rows, w2_rows = (w.rearrange("e (c p) f -> p e c f", p=P) for w in (w1, w2))
            with eng.Fori(0, E) as e:
                eng.dma_start(w1s[:, ds(e, 1)], w1_rows[:, ds(e, 1)]).then_inc(s_w, 16)
                eng.dma_start(w2s[:, ds(e, 1)], w2_rows[:, ds(e, 1)]).then_inc(s_w, 16)
                eng.wait_ge(s_w, e * 32 + 32)
                apart(eng)
            e0[0](eng)

            def prep(b, _):
                for c in range(2):
                    sp_parts(eng, b, c)
                    sp_stack(eng, b, c, ubuf(b, c))
            attention(eng, prep, lambda *a: None, lambda *a: None)
            eng.wait_ge(s_pv, 8 * 2 * B)
            with eng.Fori(0, E) as e:
                eng.dma_start(w2s[:, ds(e, 1)], w2_rows[:, ds(e, 1)]).then_inc(s_w, 16)
                eng.wait_ge(s_w, e * 16 + (32 * E + 16))
                apart(eng)
            e1[0](eng)
            with eng.Fori(0, T) as t:
                eng.wait_ge(s_comb[1], t + 1)
                apart(eng)
                eng.dma_start(out_tok[:, ds(t, 1), :], x[:, ds(t, 1), :]).then_inc(s_out, 16)
            eng.wait_ge(s_out, 16 * T)

        @block.gpsimd
        def _(eng):
            nc.gpsimd.iota(e_i[:], pattern=[[1, E]], base=0, channel_multiplier=0).then_inc(s_iota, 1)
            nc.gpsimd.iota(j_i[:], pattern=[[1, TILES]], base=0, channel_multiplier=0).then_inc(s_iota, 1)
            nc.gpsimd.memset(ident[:], 0.0).then_inc(s_iota, 1)
            nc.gpsimd.memset(ones[:], 1.0).then_inc(s_iota, 1)
            nc.gpsimd.memset(mhalf[:], -0.5).then_inc(s_const, 1)
            eng.sem_inc(r1.free, 1)
            eng.wait_ge(s_iota, 4)
            nc.gpsimd.affine_select(out=ident[:], in_=ident[:], compare_op=ALU.not_equal, fill=1.0, base=0,
                                    pattern=[[-1, P]], channel_multiplier=1).then_inc(s_const, 1)
            nc.gpsimd.affine_select(out=upper[:], in_=ones[:], compare_op=ALU.is_gt, fill=0.0, base=0,
                                    pattern=[[1, P]], channel_multiplier=-1).then_inc(s_const, 1)
            eng.wait_ge(s_const, 3)
            pool_norm(eng, r0.norm, 0)
            route0(eng, lambda g, par, more: pool_route0(eng, g, par, more))
            eng.wait_ge(s_small, SMALL)
            for c in range(DC):
                for n in range(3):
                    nc.gpsimd.tensor_copy(
                        wqkv[:, c, n, :].rearrange("p (h d) -> p h d", h=H),
                        wraw[:, c, :].rearrange("p (h n d) -> p n h d", n=3, d=DH)[:, n]).then_inc(s_sorted, 1)
            eng.wait_ge(s_sorted, 3 * DC)
            for par in range(2):
                row = 64 * par + 3 * DH
                nc.gpsimd.tensor_copy(
                    kst[:].rearrange("p u (g r) s -> p r (u g) s", r=2)[:, par],
                    ident[:, row:row + 1].unsqueeze(2).broadcast_to([P, 3 * PAIRS, S])).then_inc(s_sorted, 1)
            nc.gpsimd.memset(vs[:], 1.0).then_inc(s_sorted, 1)
            for w in range(4):
                eng.wait_ge(x0.st[w], 16 * (TILES // 4))

            pool_early(eng, 0)

            def unit(b, c, nxt, routed, early):
                if early is not None:
                    pool_early(eng, early)
                if routed is not None:
                    pool_post(eng, routed)
            attention(eng, lambda *a: None, unit, lambda *a: None)
            pool_post(eng, B - 1)
            for w in range(4):
                eng.wait_ge(x1.st[w], 16 * (TILES // 4))
            for t in range(4):
                pool_gather(eng, 1, t, t)
            with eng.Fori(1, T // 4) as it:
                for u in range(4):
                    pool_gather(eng, 1, it * 4 + u, u)

        @block.scalar
        def _(eng):
            with nc.allow_non_contiguous_dma(reason="bias columns"):
                eng.dma_start(wg[:], w_gate.rearrange("(c p) e -> p c e", p=P)).then_inc(s_wg, 16)
            act_norm(eng, r0.norm, 0)
            route0(eng, lambda g, par, more: act_route0(eng, g, par, more))
            e0[2](eng)

            attention(eng, lambda b, bb: act_prep(eng, b, bb),
                      lambda b, c, nxt, routed, early: act_unit(eng, b, c, nxt, routed),
                      lambda b, nb: act_attnT(eng, b) if nb is None else None)
            act_norm(eng, r1.norm, B - 1, bank=7)
            act_route(eng, r1, B - 1)
            e1[2](eng)

        @block.tensor
        def _(eng):
            eng.wait_ge(s_const, 3)
            eng.wait_ge(s_dve0, NCONST)
            eng.wait_ge(s_wg, 16)
            pe_norm(eng, r0.norm, 0, xn_p)
            pe_logits(eng, r0, 0)
            route0(eng, lambda g, par, more: pe_route0(eng, g, par, more))
            eng.wait_ge(s_small, SMALL)
            pe_total(eng, r0)
            e0[1](eng)
            eng.wait_ge(s_sorted, 3 * DC + 3)
            eng.wait_ge(x0.ysb, TILES)
            for done in (x0.xT, x0.relu, x0.hT):
                eng.wait_ge(done, TILES)
            eng.wait_ge(s_dve0, NCONST + 1)

            def project(b, nb):
                if nb is None:
                    eng.wait_ge(s_at, 4 * b + 3)
                    pe_heads(eng, 4 * b + 3, 1)
                    pe_attnT(eng, b)
                pe_project(eng, b)
                if nb is not None:
                    qkv_read(nb)

            def qkv_read(b):
                eng.wait_ge(s_lo, 4 * b + 4)
                eng.wait_ge(s_hi, 4 * b + 4)
                eng.wait_ge(s_vs, 2 * b + 2)

            def prep(b, bb):
                pe_prep(eng, b, bb)
                if bb is None:
                    qkv_read(b)
            attention(eng, prep, lambda b, c, nxt, routed, early: pe_unit(eng, b, c, nxt, routed), project)
            pe_norm(eng, r1.norm, B - 1, xn_p, chunks=(0,), banks=(7, 7))
            eng.wait_ge(r1.norm.ev0, B)
            pe_norm(eng, r1.norm, B - 1, xn_p, chunks=(1,), banks=(7, 7))
            pe_logits(eng, r1, B - 1)
            pe_ranks(eng, r1, B - 1)
            pe_total(eng, r1)
            e1[1](eng)

        @block.vector
        def _(eng):
            eng.wait_ge(s_iota, 2)
            nc.vector.tensor_copy(e_f[:], e_i[:]).then_inc(s_dve0, 1)
            nc.vector.tensor_copy(j_f[:], j_i[:]).then_inc(s_dve0, 1)
            nc.vector.memset(zero8[:], 0.0).then_inc(s_dve0, 1)
            nc.vector.memset(cum[:, 0, :], 0.0).then_inc(s_dve0, 1)
            nc.vector.memset(qst[:].bitcast(F32), 0.0).then_inc(s_dve0, 1)
            nc.vector.memset(mzero[:], 0.0).then_inc(s_dve0, 1)
            nc.vector.memset(ps[:, O_BANK, :], 0.0).then_inc(s_dve0, 1)
            eng.wait_ge(s_dve0, 1)
            nc.vector.tensor_scalar(e_base[:], e_f[:], float(REGION), None, ALU.mult).then_inc(s_dve0, 1)
            eng.wait_ge(s_dve0, NCONST)

            eng.wait_ge(s_x, 16)
            dve_norm(eng, r0.norm, 0, xn_p)
            dve_norm_copy(eng, r0.norm, 0)
            route0(eng, lambda g, par, more: dve_route0(eng, g, par, more))
            dve_tables(eng, r0)
            e0[3](eng)
            eng.wait_ge(x0.ysb, TILES)
            nc.vector.memset(ps[:, O_BANK, :], 0.0).then_inc(s_dve0, 1)
            eng.wait_ge(s_small, SMALL)

            for i in range(TPB):
                dve_combine(eng, 0, i, i % 2, i // 2)
            dve_early_stats(eng, 0)
            dve_early_rows(eng, 0)

            def prep(b, bb):
                dve_prep(eng, b, bb)

            def project(b, nb):
                if nb is None:
                    dve_normalise(eng, 4 * b + 3, 1, 1)
                    dve_attnT(eng, b)
                dve_project(eng, b)
            attention(eng, prep, lambda b, c, nxt, routed, early: dve_unit(eng, b, c, nxt, routed, early), project)
            dve_norm(eng, r1.norm, B - 1, xn_p, lambda: eng.wait_ge(r1.free, B))
            dve_norm_copy(eng, r1.norm, B - 1, bank=7)
            for stage in (dve_top2, dve_onehots, dve_counts, dve_weights, dve_slots):
                stage(eng, r1, B - 1)
            dve_tables(eng, r1)
            e1[3](eng)
            for t in range(4):
                dve_combine(eng, 1, t, t, 0)
            with eng.Fori(1, T // 4) as it:
                for u in range(4):
                    dve_combine(eng, 1, it * 4 + u, u, it)


_INS = ['L0_attn_X', 'L0_attn_W_qkv', 'L0_attn_b_qkv', 'L0_attn_W_out', 'L0_attn_b_out',
        'L0_ffn_Wg', 'L0_ffn_W1', 'L0_ffn_W2']


def kernel(**inputs):
    import concourse.bacc as bacc
    from concourse.bass_utils import run_bass_kernel_spmd

    nc = bacc.Bacc("TRN2", target_bir_lowering=False, num_devices=1, dynamic_dma_scratch_size=4096)
    arrays, args = {}, []
    for name in _INS:
        a = np.ascontiguousarray(inputs[name])
        arrays[f"in_{name}"] = a
        args.append(nc.dram_tensor(f"in_{name}", a.shape, mybir.dt.from_np(a.dtype), kind="ExternalInput").ap())
    shape = inputs['L0_attn_X'].shape
    args.append(nc.dram_tensor("out_0", shape, F32, kind="ExternalOutput").ap())
    macaron_kernel(nc, *args)
    r = run_bass_kernel_spmd(nc, [arrays], core_ids=[0])
    return r.results[0]["out_0"]
```
